# Optimizing a Trainium2 kernel written in Bass

```python
import numpy as np
import jax
import jax.numpy as jnp

def _softmax(x, axis=-1):
    return jax.nn.softmax(x, axis=axis)

def _gelu(x):
    return jax.nn.gelu(x, approximate=True)

def _silu(x):
    return jax.nn.silu(x)

def _sigmoid(x):
    return jax.nn.sigmoid(x)

def _layernorm(x, axis=-1, eps=1e-05):
    m = jnp.mean(x, axis=axis, keepdims=True)
    v = jnp.var(x, axis=axis, keepdims=True)
    return (x - m) / jnp.sqrt(v + eps)

def _scatter_add(tgt, idx, src, axis=0):
    return tgt.at[idx].add(src)

def _segment_sum(src, seg, n):
    return jax.ops.segment_sum(src, seg, n)
kernel_name = 'mk_gnn_resnorm_d2_gnn_r8_8383c6'

def setup_inputs(seed: int=0):
    np.random.seed(seed)
    _w = jnp.asarray

    def _rec_inputs():
        import jax
        import jax.numpy as jnp
        _gk = jax.random.key(seed)
        x = -0.0003713 + 1 * jax.random.normal(jax.random.fold_in(_gk, 1), (6250, 256), jnp.float32)
        src = jax.random.randint(jax.random.fold_in(_gk, 2), (100000,), 0, 6250, jnp.int32)
        dst = jnp.minimum((6250 * jax.random.uniform(jax.random.fold_in(_gk, 3), (100000,)) ** 2.0).astype(jnp.int32), 49999)
        _o = jnp.argsort(dst, stable=True)
        src = src[_o]
        dst = dst[_o]
        edge_weight = jax.random.uniform(jax.random.fold_in(_gk, 12), (100000,), jnp.float32, 0.0, 9.99998)
        return (x, src, dst, edge_weight)
    x, src, dst, edge_weight = _rec_inputs()

    def _L0_gnn_setup():
        import jax, jax.numpy as jnp
        import numpy as np
        CUTOFF = 10.0
        EPS_W = 1e-05
        EPS_LN = 1e-05

        def _silu(v):
            return v * jax.nn.sigmoid(v)
        key = jax.random.key(seed)
        ks = jax.random.split(key, 12)
        N, E, H, R = (6250, 37500, 256, 64)
        s = lambda fan_in: 1.0 / np.sqrt(fan_in)
        inp = {'x': jax.random.normal(ks[0], (N, H), jnp.float32), 'edge_index': jax.random.randint(ks[1], (2, E), 0, N, jnp.int64 if jax.config.jax_enable_x64 else jnp.int32), 'distances': jax.random.uniform(ks[2], (E,), jnp.float32) * CUTOFF, 'centers': jnp.linspace(0.0, CUTOFF, R).astype(jnp.float32), 'widths': jnp.full((R,), CUTOFF / R, jnp.float32), 'rbf_w1': jax.random.normal(ks[3], (R, R), jnp.float32) * s(R), 'rbf_b1': jnp.zeros((R,), jnp.float32), 'rbf_w2': jax.random.normal(ks[4], (R, R), jnp.float32) * s(R), 'rbf_b2': jnp.zeros((R,), jnp.float32), 'filt_w1': jax.random.normal(ks[5], (R, H), jnp.float32) * s(R), 'filt_b1': jnp.zeros((H,), jnp.float32), 'filt_w2': jax.random.normal(ks[6], (H, H), jnp.float32) * s(H), 'filt_b2': jnp.zeros((H,), jnp.float32), 'filt_w3': jax.random.normal(ks[7], (H, H), jnp.float32) * s(H), 'filt_b3': jnp.zeros((H,), jnp.float32), 'node_w': jax.random.normal(ks[8], (H, H), jnp.float32) * s(H), 'node_b': jnp.zeros((H,), jnp.float32), 'ln_g': jnp.ones((H,), jnp.float32), 'ln_b': jnp.zeros((H,), jnp.float32), 'gate_w': jax.random.normal(ks[9], (H, H), jnp.float32) * s(H), 'gate_b': jnp.zeros((H,), jnp.float32)}
        return inp
    _L0_gnn_all = _L0_gnn_setup()
    _L0_gnn_in = {k: v for k, v in _L0_gnn_all.items() if k in ('centers', 'widths', 'rbf_w1', 'rbf_b1', 'rbf_w2', 'rbf_b2', 'filt_w1', 'filt_b1', 'filt_w2', 'filt_b2', 'filt_w3', 'filt_b3', 'node_w', 'node_b', 'ln_g', 'ln_b', 'gate_w', 'gate_b')}
    del _L0_gnn_all

    def _L1_gnn_setup():
        import jax, jax.numpy as jnp
        import numpy as np
        N_NODES = 12500
        N_EDGES = 400000
        C = 256
        key = jax.random.key(seed)
        k1, k2, k3, k4 = jax.random.split(key, 4)
        x = jax.random.normal(k1, (N_NODES, C), dtype=jnp.float32)
        edge_weight = jax.random.uniform(k2, (N_EDGES,), dtype=jnp.float32)
        row = jax.random.randint(k3, (N_EDGES,), 0, N_NODES)
        col = jax.random.randint(k4, (N_EDGES,), 0, N_NODES)
        edge_index = jnp.stack([row, col]).astype(jnp.int64)
        return {'x': x, 'edge_weight': edge_weight, 'edge_index': edge_index}
    _L1_gnn_all = _L1_gnn_setup()
    _L1_gnn_in = {k: v for k, v in _L1_gnn_all.items() if k in ()}
    del _L1_gnn_all
    return {'x': x, 'src': src, 'dst': dst, 'edge_weight': edge_weight, 'L0_gnn_centers': _L0_gnn_in['centers'], 'L0_gnn_widths': _L0_gnn_in['widths'], 'L0_gnn_rbf_w1': _L0_gnn_in['rbf_w1'], 'L0_gnn_rbf_b1': _L0_gnn_in['rbf_b1'], 'L0_gnn_rbf_w2': _L0_gnn_in['rbf_w2'], 'L0_gnn_rbf_b2': _L0_gnn_in['rbf_b2'], 'L0_gnn_filt_w1': _L0_gnn_in['filt_w1'], 'L0_gnn_filt_b1': _L0_gnn_in['filt_b1'], 'L0_gnn_filt_w2': _L0_gnn_in['filt_w2'], 'L0_gnn_filt_b2': _L0_gnn_in['filt_b2'], 'L0_gnn_filt_w3': _L0_gnn_in['filt_w3'], 'L0_gnn_filt_b3': _L0_gnn_in['filt_b3'], 'L0_gnn_node_w': _L0_gnn_in['node_w'], 'L0_gnn_node_b': _L0_gnn_in['node_b'], 'L0_gnn_ln_g': _L0_gnn_in['ln_g'], 'L0_gnn_ln_b': _L0_gnn_in['ln_b'], 'L0_gnn_gate_w': _L0_gnn_in['gate_w'], 'L0_gnn_gate_b': _L0_gnn_in['gate_b']}

def reference(x, src, dst, edge_weight, L0_gnn_centers, L0_gnn_widths, L0_gnn_rbf_w1, L0_gnn_rbf_b1, L0_gnn_rbf_w2, L0_gnn_rbf_b2, L0_gnn_filt_w1, L0_gnn_filt_b1, L0_gnn_filt_w2, L0_gnn_filt_b2, L0_gnn_filt_w3, L0_gnn_filt_b3, L0_gnn_node_w, L0_gnn_node_b, L0_gnn_ln_g, L0_gnn_ln_b, L0_gnn_gate_w, L0_gnn_gate_b):
    import jax
    import jax.numpy as jnp

    def _L0_gnn_ref(x, edge_index, distances, centers, widths, rbf_w1, rbf_b1, rbf_w2, rbf_b2, filt_w1, filt_b1, filt_w2, filt_b2, filt_w3, filt_b3, node_w, node_b, ln_g, ln_b, gate_w, gate_b):
        import jax, jax.numpy as jnp
        import numpy as np
        CUTOFF = 10.0
        EPS_W = 1e-05
        EPS_LN = 1e-05

        def _silu(v):
            return v * jax.nn.sigmoid(v)
        d = distances
        env = 0.5 * (jnp.cos(d * jnp.pi / CUTOFF) + 1.0) * (d < CUTOFF).astype(x.dtype)
        rbf = jnp.exp(-0.5 * ((d[:, None] - centers) / (jnp.abs(widths) + EPS_W)) ** 2)
        r = rbf * env[:, None]
        r = _silu(r @ rbf_w1 + rbf_b1) @ rbf_w2 + rbf_b2
        W = _silu(r @ filt_w1 + filt_b1)
        W = _silu(W @ filt_w2 + filt_b2) @ filt_w3 + filt_b3
        row, col = (edge_index[0], edge_index[1])
        msg = (x[col] @ node_w + node_b) * W
        agg = jax.ops.segment_sum(msg, row, num_segments=x.shape[0])
        h = x + agg
        mu = jnp.mean(h, axis=-1, keepdims=True)
        var = jnp.var(h, axis=-1, keepdims=True)
        out = (h - mu) / jnp.sqrt(var + EPS_LN) * ln_g + ln_b
        return out * jax.nn.sigmoid(out @ gate_w + gate_b)

    def _L1_gnn_ref(x, edge_weight, edge_index):
        import jax, jax.numpy as jnp
        import numpy as np
        N_NODES = 12500
        N_EDGES = 400000
        C = 256
        n = x.shape[0]
        c_half = x.shape[-1] // 2
        row, col = (edge_index[0], edge_index[1])
        ones = jnp.ones(edge_index.shape[1], dtype=x.dtype)
        deg_row = jax.ops.segment_sum(ones, row, num_segments=n)
        deg_col = jax.ops.segment_sum(ones, col, num_segments=n)
        w = edge_weight[:, None]
        msg_fwd = w * x[col, :c_half]
        x_fwd = jax.ops.segment_sum(msg_fwd, row, num_segments=n)
        x_fwd = x_fwd / jnp.clip(deg_row, 1.0)[:, None]
        msg_bwd = w * x[row, c_half:]
        x_bwd = jax.ops.segment_sum(msg_bwd, col, num_segments=n)
        x_bwd = x_bwd / jnp.clip(deg_col, 1.0)[:, None]
        return jnp.concatenate([x_fwd, x_bwd], axis=-1)
    edge_index = jnp.stack([src, dst])
    x = _layernorm(x + _L0_gnn_ref(x, edge_index, edge_weight, L0_gnn_centers, L0_gnn_widths, L0_gnn_rbf_w1, L0_gnn_rbf_b1, L0_gnn_rbf_w2, L0_gnn_rbf_b2, L0_gnn_filt_w1, L0_gnn_filt_b1, L0_gnn_filt_w2, L0_gnn_filt_b2, L0_gnn_filt_w3, L0_gnn_filt_b3, L0_gnn_node_w, L0_gnn_node_b, L0_gnn_ln_g, L0_gnn_ln_b, L0_gnn_gate_w, L0_gnn_gate_b), axis=-1)
    x = _layernorm(x + _L1_gnn_ref(x, edge_weight, edge_index), axis=-1)
    return x

_drawn_inputs = setup_inputs


def setup_inputs(seed=0):
    import zlib

    import numpy as np

    out = dict(_drawn_inputs(seed))
    spreads = {'L0_gnn_widths': (0.15625, 0.6),
     'L0_gnn_rbf_b1': (0.0, 0.334),
     'L0_gnn_rbf_b2': (0.0, 0.1),
     'L0_gnn_filt_b1': (0.0, 0.1),
     'L0_gnn_filt_b2': (0.0, 0.1),
     'L0_gnn_filt_b3': (0.0, 0.1),
     'L0_gnn_node_b': (0.0, 0.1),
     'L0_gnn_ln_g': (1.0, 0.2),
     'L0_gnn_ln_b': (0.0, 0.1),
     'L0_gnn_gate_b': (0.0, 0.468)}
    factors = {'L0_gnn_centers': 3.163, 'L0_gnn_rbf_w1': 3.335}
    for name, (base, spread) in spreads.items():
        noise = np.random.default_rng([zlib.crc32(name.encode()), seed]).standard_normal(out[name].shape)
        drawn = base * np.exp(spread * noise) if base else spread * noise
        out[name] = jnp.asarray(drawn.astype(out[name].dtype))
    for name, factor in factors.items():
        out[name] = (out[name] * factor).astype(out[name].dtype)
    return out
```

```python
import math
from contextlib import ExitStack

import concourse.bass as bass
import concourse.mybir as mybir

P = 128
N = 6250
H = 256
HALF = H // 2
R = 64
NB = -(-N // P)
NP = NB * P
E = 100000
GT = 4
EC = -(-E // (P * 2 * GT)) * 2 * GT
TILES = -(-((P * EC + NB * (P - 1)) // P) // (2 * GT)) * 2 * GT
GROUPS = TILES // GT
SGROUPS = EC // GT
PAD_NODE = NP - 1
CB = 7
CHUNKS = NB // CB
ACW = HALF + 1
GW = GT * P // 2
CUTOFF = 10.0
EPS_W = 1e-5
EPS_LN = 1e-5
NV_VAR1, NV_OUT, NV_VAR2, NV = 4, 8, 13, 15
NPE = 8
NACT_STD, NACT_T, NACT_GATE, NACT_STD2, NACT = 1, 5, 9, 10, 11
FV_VAR, FV = 5, 7
ROUND = 1.5 * 2.0 ** 23


def build(nc, x, xT, src, dst, wgt, cols, rows, ln_gb, w1, w2T, f1, f2, f3, node_w, gate_w, out):
    f32, bf16, i32 = mybir.dt.float32, mybir.dt.bfloat16, mybir.dt.int32
    ALU, ACT = mybir.AluOpType, mybir.ActivationFunctionType

    y_rows = nc.dram_tensor("y_rows", (NP, H), f32).ap()
    x1_half = [nc.dram_tensor(f"x1_half{k}", (NP, HALF), f32).ap() for k in range(2)]
    records = [nc.dram_tensor(f"records{k}", (P * TILES, 4), f32).ap() for k in range(2)]
    slot_rows = nc.dram_tensor("slot_rows", (2, TILES * P), f32).ap()

    with ExitStack() as ctx:
        def sb(name, shape, dt=f32):
            return ctx.enter_context(nc.sbuf_tensor(name, shape, dt))

        def sem(name):
            return ctx.enter_context(nc.semaphore(name))

        lane = sb("lane", [P, P])
        ident = sb("ident", [P, P])
        before = sb("before", [P, P])
        ones = sb("ones", [P, P])
        ones3 = sb("ones3", [3, P], bf16)
        w1d = sb("w1d", [P, P])
        w2t = sb("w2t", [R, P])
        f1s = sb("f1s", [R, H])
        w23 = sb("w23", [P, H])
        f2s = sb("f2s", [P, 2, H])
        f3s = sb("f3s", [P, 2, H])
        nws = sb("nws", [P, 2, H])
        gws = sb("gws", [P, 2, H])
        gb = sb("gb", [P, 2, H])
        col = sb("col", [P, 8])
        negc = sb("negc", [P, 1])
        zscale = sb("zscale", [P, 1])
        b23 = sb("b23", [P, 2])
        r3 = sb("r3", [3, 3 * H])
        r3b = [sb(f"r3b{k}", [3, 3 * H]) for k in range(2)]
        part = [sb(f"part{k}", [3, 3 * H], bf16) for k in range(3)]
        bias3 = sb("bias3", [3, 3, H], bf16)

        agg = sb("agg", [P, NB * H])
        rec = [sb(f"rec{k}", [P, TILES, 4]) for k in range(2)]
        block_of = [sb(f"block_of{k}", [1, TILES], i32) for k in range(2)]
        cnt = sb("cnt", [P, NB])
        tot = sb("tot", [P, NB])
        start = sb("start", [P, NB])
        nt_i = sb("nt_i", [P, NB], i32)
        offs = sb("offs", [P, NB])
        ntc = sb("ntc", [NB, 1])
        ntc_i = sb("ntc_i", [NB, 1], i32)
        startc = sb("startc", [NB, 1])

        A1 = 17 * EC
        arena1 = sb("arena1", [P, A1])
        at = 0

        def take(n):
            nonlocal at
            at += n
            return arena1[:, at - n:at]

        stage_rec = [take(4 * EC) for _ in range(2)]
        stage_adr = [take(EC).bitcast(i32) for _ in range(2)]
        key_i = [take(EC).bitcast(i32) for _ in range(2)]
        wt = take(EC)
        blk, eq, run, rank = take(EC), take(EC), take(EC), take(EC)
        acc = [arena1[:, k * NB * ACW:(k + 1) * NB * ACW] for k in range(2)]

        chunk = [arena1[:, k * CB * H:(k + 1) * CB * H] for k in range(7)]

        arena2 = sb("arena2", [P, 33 * GW])
        at2 = 0

        def ring(*shape):
            nonlocal at2
            n = math.prod(shape)
            v = arena2[:, at2:at2 + n]
            at2 += n
            if len(shape) == 2:
                v = v.rearrange("p (a b) -> p a b", a=shape[0])
            if len(shape) == 3:
                v = v.rearrange("p (a b c) -> p a b c", a=shape[0], b=shape[1])
            return v

        gath = [ring(GT, H) for _ in range(2)]
        de = [ring(2, GW) for _ in range(2)]
        sq = ring(GW)
        th = [ring(GW) for _ in range(2)]
        up1 = ring(GW)
        rcp = ring(GW)
        rbf = [ring(GW) for _ in range(2)]
        s1 = [ring(GW) for _ in range(2)]
        s2 = ring(2, GT * P)
        s3 = ring(2, GT * P)
        msg = ring(GT, H)
        assert at2 == 33 * GW and 17 * EC >= 7 * CB * H
        last_c = [arena2[:, k * CB * H:(k + 1) * CB * H] for k in range(3)]
        xt_c = last_c[0].rearrange("p (k n) -> p k n", k=2)
        y_c = last_c[1].rearrange("p (j n) -> p j n", j=CB)
        tile_no = arena2[:, 2 * CB * H:2 * CB * H + TILES]
        reached = arena2[0:NB, 2 * CB * H + TILES:2 * CB * H + 2 * TILES]
        rows_of_slots = arena2[:, at2 - 2 * CB * P:at2].rearrange("p (a b c) -> p a b c", a=2, b=CB)
        msg2 = [(s2, s3)[k].rearrange("p a b -> p (a b)")[:, 0:GT * ACW].rearrange("p (t f) -> p t f", t=GT)
                for k in range(2)]
        hot = [sb(f"hot{k}", [P, GT, P]) for k in range(2)]
        idx = [sb(f"idx{k}", [P, GT], i32) for k in range(2)]
        sc_rec = [sb(f"sc_rec{k}", [P, GT, 4]) for k in range(2)]
        sc_adr = [sb(f"sc_adr{k}", [P, GT], i32) for k in range(2)]
        stats = sb("stats", [P, CB, 6])
        mv = sb("mv", [P, CB, 2])
        var_eps = sb("var_eps", [P, CB])
        std = sb("std", [P, CB])
        rstd = sb("rstd", [P, CB])
        rdeg = [sb(f"rdeg{k}", [P, NB]) for k in range(2)]

        ps = ctx.enter_context(nc.psum_tensor("ps", [P, 8, 512], f32))

        edges_in, weights_in = sem("edges_in"), sem("weights_in")
        default_set, default_out = sem("default_set"), sem("default_out")
        consts = sem("consts")
        carrier = sem("carrier")
        fused_mm, params_set, biases_set = sem("fused_mm"), sem("params_set"), sem("biases_set")
        counted, prefix_mm, tiles_set = sem("counted"), sem("prefix_mm"), sem("tiles_set")
        starts_mm, reached_set, table_mm, table_set = (
            sem("starts_mm"), sem("reached_set"), sem("table_mm"), sem("table_set"))
        envelope = sem("envelope")
        chain = sem("chain")
        sorted_key = sem("sorted_key")
        xt_in, y_mm, y_evac, y_out = sem("xt_in"), sem("y_mm"), sem("y_evac"), sem("y_out")
        sc_staged = sem("sc_staged")
        scattered = [[sem(f"scattered{k}{b}") for b in range(2)] for k in range(2)]
        rec_in = [sem(f"rec_in{k}") for k in range(2)]
        rows_mm, rows_evac, rows_out = sem("rows_mm"), sem("rows_evac"), sem("rows_out")
        de_in = [sem(f"de_in{b}") for b in range(2)]
        squared, tanh_done, rbf_done = sem("squared"), sem("tanh_done"), sem("rbf_done")
        rbf_chain = sem("rbf_chain")
        l1_mm, l23_mm, l4_mm, l5_mm = sem("l1_mm"), sem("l23_mm"), sem("l4_mm"), sem("l5_mm")
        s1_done, s2_done, s3_done = sem("s1_done"), sem("s2_done"), sem("s3_done")
        idx_staged = sem("idx_staged")
        gathered = [sem(f"gathered{b}") for b in range(2)]
        hot_done, msg_done, agg_mm, added = sem("hot_done"), sem("msg_done"), sem("agg_mm"), sem("added")
        x_in, nv, npe, nact, x1_out = sem("x_in"), sem("nv"), sem("npe"), sem("nact"), sem("x1_out")
        idx2_staged = sem("idx2_staged")
        gathered2 = [sem(f"gathered2{b}") for b in range(2)]
        hot2_done, scaled, agg2_mm, added2 = sem("hot2_done"), sem("scaled"), sem("agg2_mm"), sem("added2")
        fv, fact, out_done = sem("fv"), sem("fact"), sem("out_done")

        block = ctx.enter_context(nc.Block())

        y_v = y_rows.rearrange("(c j p) n -> c p j n", p=P, j=CB)
        x_v = x.rearrange("(c j p) n -> c p j n", p=P, j=CB)
        out_v = out.rearrange("(c j p) n -> c p j n", p=P, j=CB)
        x1_v = [t.rearrange("(c j p) n -> c p j n", p=P, j=CB) for t in x1_half]
        xT_v = xT.rearrange("(k p) (c n) -> c p k n", p=P, c=CHUNKS)
        rec_v = [t.rearrange("(p t) f -> p t f", p=P) for t in records]

        def hold(eng, s, value):
            eng.wait_ge(s, value)
            eng.sem_inc(carrier)

        def pairs(eng, body, lo, hi):
            with eng.Fori((lo + 1) // 2, hi // 2 + 1) as i:
                body(2 * i - 1, i - 1, 1)
                body(2 * i, i, 0)

        def chunks(eng, body):
            body(0)
            with eng.Fori(1, CHUNKS) as c:
                body(c)

        def single(body, *groups):
            for g in groups:
                body(g, g // 2, g % 2)

        n_weights = 12

        @block.sync
        def _(sp):
            for t, d in ((key_i[0], src), (key_i[1], dst), (wt, wgt)):
                sp.dma_start(t, d).then_inc(edges_in, 16)
            for t, d in ((w2t, w2T), (f1s, f1), (col, cols), (r3, rows)):
                sp.dma_start(t[:, :], d).then_inc(weights_in, 16)
            for t, d in ((f2s, f2), (f3s, f3), (nws, node_w), (gws, gate_w)):
                sp.dma_start(t[:, :, :], d.rearrange("(k p) n -> p k n", p=P)).then_inc(weights_in, 16)
            for k in range(2):
                sp.dma_start(gb[:, k, :], ln_gb[k:k + 1, :].to_broadcast([P, H])).then_inc(weights_in, 16)
            sp.wait_ge(default_set, 5)
            for h in range(2):
                sp.dma_start(w1d[h * R:(h + 1) * R, h * R:(h + 1) * R], w1).then_inc(weights_in, 16)
            for k in range(2):
                sp.dma_start(rec_v[k], rec[0][:, :, :]).then_inc(default_out, 16)

            def y_step(c):
                sp.dma_start(xt_c, xT_v[c]).then_inc(xt_in, 16)
                sp.wait_ge(y_evac, 4 * c + 4)
                sp.dma_start(y_v[c], y_c).then_inc(y_out, 16)

            with sp.Fori(0, CHUNKS) as c:
                y_step(c)
            sp.wait_ge(y_out, 16 * CHUNKS)

            for b in range(2):
                sp.wait_ge(scattered[0][b], 16 * GT * (SGROUPS // 2))
            sp.dma_start(rec[0][:, :, :], rec_v[0]).then_inc(rec_in[0], 16)
            for f in range(2):
                sp.wait_ge(rows_evac, 3 * (f + 1))
                sp.dma_start(slot_rows[f, 0:6 * P * P].rearrange("(j t l) -> t j l", t=P, l=P),
                             rows_of_slots[:, f, 0:6, :]).then_inc(rows_out, 16)
                sp.dma_start(slot_rows[f, 6 * P * P:TILES * P].rearrange("(t l) -> t l", l=P),
                             rows_of_slots[0:TILES - 6 * P, f, 6, :]).then_inc(rows_out, 16)
            sp.wait_ge(rows_out, 64)

            def load_de(g, q, b):
                if not (isinstance(g, int) and g < 2):
                    sp.wait_ge(rbf_done, g - 1)
                for f in range(2):
                    for h in range(2):
                        sp.dma_start(de[b][h * R:(h + 1) * R, f, :],
                                     slot_rows[f:f + 1, bass.ds(g * (GT * P) + h * GW, GW)].to_broadcast([R, GW])
                                     ).then_inc(de_in[b], 16)

            single(load_de, 0, 1, 2)
            pairs(sp, load_de, 3, 204)
            single(load_de, 205, 206, 207)

            for b in range(2):
                sp.wait_ge(scattered[1][b], 16 * GT * (SGROUPS // 2))
            sp.dma_start(rec[1][:, :, :], rec_v[1]).then_inc(rec_in[1], 16)

            with sp.Fori(0, CHUNKS) as c:
                sp.dma_start(chunk[0].rearrange("p (j n) -> p j n", j=CB), x_v[c]).then_inc(x_in, 16)
                sp.wait_ge(nv, NV * c + NV)
                for k in range(2):
                    sp.dma_start(x1_v[k][c], chunk[5].rearrange("p (j n) -> p j n", j=CB)
                                 [:, :, k * HALF:(k + 1) * HALF]).then_inc(x1_out, 16)

            with sp.Fori(0, CHUNKS) as c:
                sp.wait_ge(fv, FV * c + FV)
                sp.dma_start(out_v[c], last_c[2].rearrange("p (j n) -> p j n", j=CB)).then_inc(out_done, 16)
            sp.wait_ge(out_done, 16 * CHUNKS)

        @block.gpsimd
        def _(pool):
            nc.gpsimd.iota(lane[:, :], [[1, P]], base=0, channel_multiplier=0,
                           allow_small_or_imprecise_dtypes=True).then_inc(consts, 1)
            nc.gpsimd.iota(tile_no, [[1, TILES]], base=0, channel_multiplier=0,
                           allow_small_or_imprecise_dtypes=True).then_inc(consts, 1)
            nc.gpsimd.memset(ones[:, :], 1.0).then_inc(consts, 1)
            nc.gpsimd.memset(ones3[:, :], 1.0).then_inc(consts, 1)
            pool.wait_ge(consts, 4)
            nc.gpsimd.affine_select(out=before[:, :], in_=ones[:, :], compare_op=ALU.is_gt, fill=0.0,
                                    base=0, pattern=[[1, P]], channel_multiplier=-1).then_inc(consts, 1)
            nc.gpsimd.affine_select(out=ident[:, :], in_=ones[:, :], compare_op=ALU.is_equal, fill=0.0,
                                    base=0, pattern=[[1, P]], channel_multiplier=-1).then_inc(consts, 1)

            def scatter(k):
                def body(g, q, b):
                    hold(pool, sc_staged, 2 * g + 2 + 2 * SGROUPS * k)
                    for t in range(GT):
                        pool.indirect_dma_start(
                            records[k], bass.IndirectOffsetOnAxis(ap=sc_adr[b][:, t:t + 1], axis=0),
                            sc_rec[b][:, t, :], None).then_inc(scattered[k][b], 16)
                return body

            def gather(g, q, b):
                hold(pool, idx_staged, g + 1)
                if not (isinstance(g, int) and g < 2):
                    hold(pool, msg_done, 2 * g - 2)
                for t in range(GT):
                    pool.indirect_dma_start(
                        gath[b][:, t, :], None, y_rows,
                        bass.IndirectOffsetOnAxis(ap=idx[b][:, t:t + 1], axis=0)).then_inc(gathered[b], 16)

            pool.wait_ge(default_out, 32)
            single(scatter(0), 0, 1, 2)
            pairs(pool, scatter(0), 3, SGROUPS - 2)
            single(scatter(0), SGROUPS - 1)

            def gather_scatter(g, q, b):
                gather(g, q, b)
                scatter(1)(g, q, b)

            pool.wait_ge(y_out, 16 * CHUNKS)
            single(gather_scatter, 0, 1, 2)
            pairs(pool, gather_scatter, 3, SGROUPS - 2)
            single(gather_scatter, SGROUPS - 1)
            single(gather, SGROUPS)
            pairs(pool, gather, SGROUPS + 1, 204)
            single(gather, 205, 206, 207)

            pool.wait_ge(x1_out, 32 * CHUNKS)
            for k in range(2):
                def gather2(g, q, b):
                    hold(pool, idx2_staged, g + 1 + GROUPS * k)
                    if k or not (isinstance(g, int) and g < 2):
                        hold(pool, scaled, g - 1 + GROUPS * k)
                    for t in range(GT):
                        pool.indirect_dma_start(
                            gath[b][:, t, 0:HALF], None, x1_half[k],
                            bass.IndirectOffsetOnAxis(ap=idx[b][:, t:t + 1], axis=0)).then_inc(gathered2[b], 16)
                single(gather2, 0, 1, 2)
                pairs(pool, gather2, 3, 204)
                single(gather2, 205, 206, 207)

        @block.scalar
        def _(act):
            act.wait_ge(envelope, 1)
            nc.scalar.activation(run, eq, ACT.Sin).then_inc(envelope, 1)

            def y_evacuate(c):
                if not isinstance(c, int):
                    act.wait_ge(y_out, 16 * c)
                for j in range(4):
                    w = 2 if j < 3 else 1
                    act.wait_ge(y_mm, 4 * c + j + 1)
                    nc.scalar.activation(y_c[:, 2 * j:2 * j + w, :].rearrange("p a b -> p (a b)"),
                                         ps[:, j, 0:w * H], ACT.Copy).then_inc(y_evac, 1)

            chunks(act, y_evacuate)

            def stage(k):
                def body(g, q, b):
                    if not (isinstance(g, int) and g < 2):
                        hold(act, scattered[k][b], 16 * GT * q)
                    nc.scalar.activation(sc_rec[b][:, :, :].rearrange("p a b -> p (a b)"),
                                         stage_rec[k][:, bass.ds(g * (4 * GT), 4 * GT)],
                                         ACT.Copy).then_inc(sc_staged, 1)
                    nc.scalar.activation(sc_adr[b][:, :], stage_adr[k][:, bass.ds(g * GT, GT)],
                                         ACT.Copy).then_inc(sc_staged, 1)
                return body

            act.wait_ge(sorted_key, 1)
            single(stage(0), 0, 1, 2)
            pairs(act, stage(0), 3, SGROUPS - 2)
            single(stage(0), SGROUPS - 1)

            for f in range(2):
                act.wait_ge(rows_mm, 7 * (f + 1))
                nc.scalar.activation(rows_of_slots[:, f, 0:4, :].rearrange("p a b -> p (a b)"),
                                     ps[:, 2 * f, :], ACT.Copy).then_inc(rows_evac, 1)
                nc.scalar.activation(rows_of_slots[:, f, 4:6, :].rearrange("p a b -> p (a b)"),
                                     ps[:, 2 * f + 1, 0:2 * P], ACT.Copy).then_inc(rows_evac, 1)
                nc.scalar.activation(rows_of_slots[0:TILES - 6 * P, f, 6, :],
                                     ps[0:TILES - 6 * P, 2 * f + 1, 2 * P:3 * P], ACT.Copy).then_inc(rows_evac, 1)

            def radial(g, q, b):
                act.wait_ge(de_in[b], 64 * q + 64)
                if not (isinstance(g, int) and g == 0):
                    act.wait_ge(tanh_done, g)
                nc.scalar.activation(sq, de[b][:, 0, :], ACT.Square, bias=negc[:, 0:1]).then_inc(squared, 1)
                act.wait_ge(squared, g + 1)
                nc.scalar.activation(th[b], sq, ACT.Tanh, scale=zscale[:, 0:1]).then_inc(tanh_done, 1)

            def silu1(g, q, b):
                act.wait_ge(l1_mm, g + 1)
                nc.scalar.activation(s1[b], ps[:, 0, 0:GW], ACT.Silu,
                                     bias=col[:, 2:3]).then_inc(s1_done, 1)

            def silu2(g):
                act.wait_ge(l23_mm, g + 1)
                for m in range(2):
                    nc.scalar.activation(s2[:, m, :].rearrange("p (h e) -> p h e", h=2),
                                         ps[:, 1:3, m * GW:(m + 1) * GW], ACT.Silu,
                                         bias=b23[:, m:m + 1]).then_inc(s2_done, 1)

            def silu3(g):
                for m in range(2):
                    act.wait_ge(l4_mm, 2 * g + m + 1)
                    nc.scalar.activation(s3[:, m, :], ps[:, 3 + m, :], ACT.Silu,
                                         bias=col[:, 5 + m:6 + m]).then_inc(s3_done, 1)

            def stage_idx(g, q, b):
                if not (isinstance(g, int) and g < 2):
                    hold(act, gathered[b], 16 * GT * q)
                nc.scalar.activation(idx[b][:, :], rec[0][:, bass.ds(g * GT, GT), 1],
                                     ACT.Copy).then_inc(idx_staged, 1)

            def act_group(scatters, ahead=2):
                def body(g, q, b):
                    silu2(g)
                    if ahead == 2:
                        radial(g + 2, q + 1, b)
                    if ahead:
                        stage_idx(g + 1, q + b, 1 - b)
                    if scatters:
                        stage(1)(g, q, b)
                    silu3(g)
                    if ahead:
                        silu1(g + 1, q + b, 1 - b)
                return body

            act.wait_ge(weights_in, 16 * n_weights)
            act.wait_ge(params_set, 2)
            act.wait_ge(rec_in[0], 16)
            act.wait_ge(sorted_key, 2)
            radial(0, 0, 0)
            radial(1, 0, 1)
            stage_idx(0, 0, 0)
            silu1(0, 0, 0)
            single(act_group(True), 0, 1, 2)
            pairs(act, act_group(True), 3, SGROUPS - 2)
            single(act_group(True), SGROUPS - 1)
            single(act_group(False), SGROUPS)
            pairs(act, act_group(False), SGROUPS + 1, 204)
            single(act_group(False), 205)
            single(act_group(False, 1), 206)
            single(act_group(False, 0), 207)

            with act.Fori(0, CHUNKS) as c:
                act.wait_ge(nv, NV * c + NV_VAR1)
                nc.scalar.activation(std[:, :], var_eps[:, :], ACT.Sqrt).then_inc(nact, 1)
                for j in range(4):
                    w = 4 * P if j < 3 else 2 * P
                    act.wait_ge(npe, NPE * c + j + 1)
                    nc.scalar.activation(chunk[3][:, j * 4 * P:j * 4 * P + w], ps[:, j, 0:w],
                                         ACT.Copy).then_inc(nact, 1)
                for j in range(4):
                    w = 2 * H if j < 3 else H
                    act.wait_ge(npe, NPE * c + 4 + j + 1)
                    nc.scalar.activation(chunk[4][:, j * 2 * H:j * 2 * H + w], ps[:, 4 + j, 0:w],
                                         ACT.Tanh, scale=0.5).then_inc(nact, 1)
                act.wait_ge(nv, NV * c + NV_VAR2)
                nc.scalar.activation(std[:, :], var_eps[:, :], ACT.Sqrt).then_inc(nact, 1)
                hold(act, nv, NV * c + NV)
                nc.scalar.activation(agg[:, bass.ds(c * (CB * H), CB * H)], chunk[5],
                                     ACT.Copy).then_inc(nact, 1)

            act.wait_ge(rec_in[1], 16)
            for k in range(2):
                def stage_idx2(g, q, b):
                    if k or not (isinstance(g, int) and g < 2):
                        hold(act, gathered2[b], 16 * GT * (q + GROUPS // 2 * k))
                    nc.scalar.activation(idx[b][:, :], rec[k][:, bass.ds(g * GT, GT), 1],
                                         ACT.Copy).then_inc(idx2_staged, 1)
                single(stage_idx2, 0, 1, 2)
                pairs(act, stage_idx2, 3, 204)
                single(stage_idx2, 205, 206, 207)

            with act.Fori(0, CHUNKS) as c:
                act.wait_ge(fv, FV * c + FV_VAR)
                nc.scalar.activation(std[:, :], var_eps[:, :], ACT.Sqrt).then_inc(fact, 1)

        @block.tensor
        def _(pe):
            mm = nc.tensor.matmul
            pe.wait_ge(weights_in, 16 * n_weights)
            pe.wait_ge(consts, 6)
            mm(ps[:, 4, 0:H], w2t[:, :], f1s[:, :], start=True, stop=True)
            for m in range(2):
                last = mm(ps[:, 5, m:m + 1], f1s[:, m * P:(m + 1) * P], col[0:R, 7:8], start=True, stop=True)
            last.then_inc(fused_mm, 1)
            pe.wait_ge(biases_set, 1)

            def y_product(c):
                pe.wait_ge(xt_in, 16 * c + 16)
                for j in range(CB):
                    if j % 2 == 0 and not isinstance(c, int):
                        pe.wait_ge(y_evac, 4 * c + j // 2 - 3)
                    o = ps[:, j // 2, (j % 2) * H:(j % 2 + 1) * H]
                    for k in range(2):
                        mm(o, xt_c[:, k, j * P:(j + 1) * P], nws[:, k, :], start=(k == 0), stop=False)
                    last = mm(o, ones3[:, :], bias3[:, 1, :], start=False, stop=True)
                    if j % 2 or j == CB - 1:
                        last.then_inc(y_mm, 1)

            chunks(pe, y_product)

            for k in range(2):
                pe.wait_ge(counted, k + 1)
                mm(ps[:, 6, 0:NB], before[:, :], cnt[:, :], start=True, stop=True)
                mm(ps[:, 6, 64:64 + NB], ones[:, :], cnt[:, :], start=True, stop=True)
                mm(ps[0:NB, 6, 128:129], cnt[:, :], ones[:, 0:1], start=True, stop=True).then_inc(prefix_mm, 1)
                pe.wait_ge(tiles_set, k + 1)
                mm(ps[0:NB, 6, 130:131], before[0:NB, 0:NB], ntc[:, :], start=True, stop=True).then_inc(starts_mm, 1)
                pe.wait_ge(reached_set, k + 1)
                for h in range(2):
                    last = mm(ps[0:1, 5 + 2 * h, 0:TILES // 2], ones[0:NB, 0:1],
                              reached[:, h * (TILES // 2):(h + 1) * (TILES // 2)], start=True, stop=True)
                last.then_inc(table_mm, 1)
                pe.wait_ge(table_set, k + 1)

            pe.wait_ge(rec_in[0], 16)
            pe.wait_ge(y_evac, 4 * CHUNKS)
            for f in range(2):
                for j in range(7):
                    w = P if j < 6 else TILES - 6 * P
                    nc.tensor.transpose(ps[0:w, 2 * f + j // 4, (j % 4) * P:(j % 4 + 1) * P],
                                        rec[0][:, j * P:j * P + w, 2 + f], ident[:, :]).then_inc(rows_mm, 1)

            def layer1(g, q, b):
                pe.wait_ge(rbf_done, g + 1)
                if not (isinstance(g, int) and g < 3):
                    pe.wait_ge(added, 4 * g - 8)
                mm(ps[:, 0, 0:GW], w1d[:, :], rbf[b], start=True, stop=True).then_inc(l1_mm, 1)

            def layer23(g, q, b):
                pe.wait_ge(s1_done, g + 1)
                for m in range(2):
                    for h in range(2):
                        last = mm(ps[:, 1 + h, m * GW:(m + 1) * GW],
                                  w23[h * R:(h + 1) * R, m * P:(m + 1) * P],
                                  s1[b][h * R:(h + 1) * R, :], start=True, stop=True)
                last.then_inc(l23_mm, 1)

            def layer4(g):
                pe.wait_ge(s2_done, 2 * g + 2)
                for m in range(2):
                    for k in range(2):
                        last = mm(ps[:, 3 + m, :], f2s[:, k, m * P:(m + 1) * P], s2[:, k, :],
                                  start=(k == 0), stop=(k == 1))
                    last.then_inc(l4_mm, 1)

            def layer5(g):
                pe.wait_ge(s3_done, 2 * g + 2)
                for t in range(GT):
                    if t % 2 == 0 and not (isinstance(g, int) and g < 1):
                        pe.wait_ge(msg_done, 2 * g + t // 2 - 1)
                    o = ps[:, 5 + t // 2, (t % 2) * H:(t % 2 + 1) * H]
                    for k in range(2):
                        mm(o, s3[:, k, t * P:(t + 1) * P], f3s[:, k, :], start=(k == 0), stop=False)
                    last = mm(o, ones3[:, :], bias3[:, 0, :], start=False, stop=True)
                    if t % 2:
                        last.then_inc(l5_mm, 1)

            def aggregate(g, b):
                pe.wait_ge(hot_done, g + 1)
                for h in range(2):
                    pe.wait_ge(msg_done, 2 * g + h + 1)
                    if not (isinstance(g, int) and g == 0):
                        pe.wait_ge(added, 4 * g - 2 + 2 * h)
                    if h:
                        pe.wait_ge(s1_done, min(g + 3, GROUPS) if isinstance(g, int) else g + 3)
                    for t in (2 * h, 2 * h + 1):
                        last = mm(ps[:, 7 * (1 - h), (t % 2) * H:(t % 2 + 1) * H], hot[b][:, t, :], msg[:, t, :],
                                  start=True, stop=True)
                    last.then_inc(agg_mm, 1)

            def pe_group(g, q, b, before_it=True, after_it=True):
                layer23(g, q, b)
                if before_it:
                    layer5(g - 1)
                layer4(g)
                if after_it:
                    layer1(g + 1, q + b, 1 - b)
                if before_it:
                    aggregate(g - 1, 1 - b)

            layer1(0, 0, 0)
            pe_group(0, 0, 0, before_it=False)
            single(pe_group, 1, 2)
            pairs(pe, pe_group, 3, 204)
            single(pe_group, 205, 206)
            pe_group(207, 103, 1, after_it=False)
            layer5(207)
            aggregate(207, 1)

            with pe.Fori(0, CHUNKS) as c:
                pe.wait_ge(nv, NV * c + NV_OUT)
                for j in range(2 * CB):
                    last = nc.tensor.transpose(ps[:, j // 4, (j % 4) * P:(j % 4 + 1) * P],
                                               chunk[2][:, j * P:(j + 1) * P], ident[:, :])
                    if j % 4 == 3 or j == 2 * CB - 1:
                        last.then_inc(npe, 1)
                for j in range(CB):
                    if j % 2 == 0:
                        pe.wait_ge(nact, NACT * c + NACT_STD + j // 2 + 1)
                    o = ps[:, 4 + j // 2, (j % 2) * H:(j % 2 + 1) * H]
                    for k in range(2):
                        mm(o, chunk[3][:, (2 * j + k) * P:(2 * j + k + 1) * P], gws[:, k, :],
                           start=(k == 0), stop=False)
                    last = mm(o, ones3[:, :], bias3[:, 2, :], start=False, stop=True)
                    if j % 2 or j == CB - 1:
                        last.then_inc(npe, 1)

            for k in range(2):
                def aggregate2(g, q, b):
                    pe.wait_ge(hot2_done, g + 1 + GROUPS * k)
                    pe.wait_ge(scaled, g + 1 + GROUPS * k)
                    if k or not (isinstance(g, int) and g < 2):
                        pe.wait_ge(added2, GT * (g - 1) + GT * GROUPS * k)
                    for t in range(GT):
                        last = mm(ps[:, 2 * b + t // 2, (t % 2) * H:(t % 2) * H + ACW], hot[b][:, t, :],
                                  msg2[b][:, t, :], start=True, stop=True)
                        if t % 2:
                            last.then_inc(agg2_mm, 1)
                single(aggregate2, 0, 1, 2)
                pairs(pe, aggregate2, 3, 204)
                single(aggregate2, 205, 206, 207)

        @block.vector
        def _(dve):
            V = nc.vector

            def stepper(s, start=0):
                n = [0]

                def step(ins):
                    n[0] += 1
                    ins.then_inc(s, 1)
                    dve.wait_ge(s, start + n[0])
                step.count = n
                return step


            for f, v in enumerate((-1.0, float(PAD_NODE), 0.0, 0.0)):
                V.memset(rec[0][:, :, f], v).then_inc(default_set, 1)
            V.memset(w1d[:, :], 0.0).then_inc(default_set, 1)
            V.memset(agg[:, :], 0.0)

            step = stepper(chain)
            dve.wait_ge(edges_in, 48)
            step(V.tensor_scalar(run, wt, 0.5 / CUTOFF, None, ALU.mult))
            step(V.scalar_tensor_tensor(eq, run, -1.0, run, ALU.mult, ALU.max))
            step(V.tensor_scalar(run, eq, ROUND, None, ALU.add))
            step(V.tensor_scalar(run, run, -ROUND, None, ALU.add))
            step(V.tensor_tensor(eq, eq, run, ALU.subtract))
            step(V.scalar_tensor_tensor(run, eq, -1.0, eq, ALU.mult, ALU.max))
            V.tensor_scalar(eq, run, -2.0 * math.pi, 0.5 * math.pi, ALU.mult, ALU.add).then_inc(envelope, 1)
            step(V.tensor_scalar(blk, wt, CUTOFF, None, ALU.is_lt))
            srec = [t.rearrange("p (e f) -> p e f", f=4) for t in stage_rec]
            dve.wait_ge(envelope, 2)
            step(V.scalar_tensor_tensor(srec[0][:, :, 3], run, 1.0, blk, ALU.add, ALU.mult))
            V.memset(srec[1][:, :, 3], 0.0)

            def sort_key(k):
                step(V.tensor_scalar(eq.bitcast(i32), key_i[k], 7, None, ALU.logical_shift_right))
                step(V.tensor_copy(blk, eq.bitcast(i32)))
                step(V.tensor_scalar(run.bitcast(i32), key_i[k], P - 1, None, ALU.bitwise_and))
                V.tensor_copy(srec[k][:, :, 0], run.bitcast(i32))
                V.tensor_copy(srec[k][:, :, 1], key_i[1 - k])
                step(V.tensor_copy(srec[k][:, :, 2], wt))
                done = step.count[0]
                with dve.Fori(0, NB) as b:
                    stepper(chain, done + b)(
                        V.tensor_scalar(run, blk, lane[:, bass.ds(b, 1)], None, ALU.is_equal, ALU.add,
                                        accum_out=cnt[:, bass.ds(b, 1)]))
                step.count[0] += NB
                V.memset(rank, 0.0).then_inc(counted, 1)
                dve.wait_ge(prefix_mm, k + 1)
                step(V.tensor_scalar(nt_i[:, :], ps[:, 6, 64:64 + NB], float(P - 1), None, ALU.add))
                step(V.tensor_scalar(nt_i[:, :], nt_i[:, :], 7, None, ALU.logical_shift_right))
                step(V.tensor_copy(tot[:, :], nt_i[:, :]))
                step(V.tensor_tensor_scan(start[:, :], tot[:, :], tot[:, :], 0.0, ALU.add, ALU.max))
                step(V.tensor_tensor(start[:, :], start[:, :], tot[:, :], ALU.subtract))
                step(V.scalar_tensor_tensor(offs[:, :], start[:, :], float(P), ps[:, 6, 0:NB], ALU.mult, ALU.add))
                step(V.tensor_scalar(ntc_i[:, :], ps[0:NB, 6, 128:129], float(P - 1), None, ALU.add))
                step(V.tensor_scalar(ntc_i[:, :], ntc_i[:, :], 7, None, ALU.logical_shift_right))
                V.tensor_copy(ntc[:, :], ntc_i[:, :]).then_inc(tiles_set, 1)
                dve.wait_ge(starts_mm, k + 1)
                step(V.tensor_copy(startc[:, :], ps[0:NB, 6, 130:131]))
                V.tensor_scalar(reached, tile_no[0:NB], startc[:, 0:1], None,
                                ALU.is_ge).then_inc(reached_set, 1)
                dve.wait_ge(table_mm, k + 1)
                for h in range(2):
                    last = V.tensor_scalar(block_of[k][:, h * (TILES // 2):(h + 1) * (TILES // 2)],
                                           ps[0:1, 5 + 2 * h, 0:TILES // 2], -1.0, None, ALU.add)
                last.then_inc(table_set, 1)
                done = step.count[0]
                with dve.Fori(0, NB) as b:
                    turn = stepper(chain, done + 4 * b)
                    turn(V.tensor_scalar(eq, blk, lane[:, bass.ds(b, 1)], None, ALU.is_equal))
                    turn(V.tensor_tensor_scan(run, eq, eq, offs[:, bass.ds(b, 1)], ALU.add, ALU.max))
                    turn(V.tensor_tensor(run, run, eq, ALU.mult))
                    turn(V.tensor_tensor(rank, rank, run, ALU.add))
                step.count[0] += 4 * NB
                slot_i, lane_i, tile_i = eq.bitcast(i32), run.bitcast(i32), blk.bitcast(i32)
                step(V.tensor_scalar(slot_i, rank, -1.0, None, ALU.add))
                step(V.tensor_scalar(lane_i, slot_i, P - 1, None, ALU.bitwise_and))
                step(V.tensor_scalar(tile_i, slot_i, 7, None, ALU.logical_shift_right))
                V.scalar_tensor_tensor(stage_adr[k], lane_i, float(TILES), tile_i,
                                       ALU.mult, ALU.add).then_inc(sorted_key, 1)

            dve.wait_ge(consts, 6)
            dve.wait_ge(weights_in, 16 * n_weights)
            V.tensor_scalar(negc[:, :], col[:, 0:1], -1.0, None, ALU.mult)
            step(V.scalar_tensor_tensor(zscale[:, :], col[:, 1:2], -1.0, col[:, 1:2], ALU.mult, ALU.max))
            step(V.tensor_scalar(zscale[:, :], zscale[:, :], EPS_W, None, ALU.add))
            step(V.reciprocal(zscale[:, :], zscale[:, :]))
            step(V.tensor_tensor(zscale[:, :], zscale[:, :], zscale[:, :], ALU.mult))
            V.tensor_scalar(zscale[:, :], zscale[:, :], 0.25, None, ALU.mult).then_inc(params_set, 1)
            dve.wait_ge(fused_mm, 1)
            V.tensor_copy(w23[:, :], ps[:, 4, 0:H])
            V.tensor_tensor(b23[:, :], ps[:, 5, 0:2], col[:, 3:5], ALU.add).then_inc(params_set, 1)
            step(V.tensor_copy(part[0][:, :], r3[:, :]))
            step(V.tensor_tensor(r3b[0][:, :], r3[:, :], part[0][:, :], ALU.subtract))
            step(V.tensor_copy(part[1][:, :], r3b[0][:, :]))
            step(V.tensor_tensor(r3b[1][:, :], r3b[0][:, :], part[1][:, :], ALU.subtract))
            step(V.tensor_copy(part[2][:, :], r3b[1][:, :]))
            step(V.tensor_scalar(r3b[0][:, :], part[0][:, :], ident[0:3, 0:1], None, ALU.mult))
            for k in (1, 2):
                o = r3b[1][:, :] if k == 1 else bias3[:, :, :].rearrange("p a b -> p (a b)")
                i = r3b[0][:, :] if k == 1 else r3b[1][:, :]
                last = V.scalar_tensor_tensor(o, part[k][:, :], ident[0:3, k:k + 1], i, ALU.mult, ALU.add)
                if k == 1:
                    step(last)
            last.then_inc(biases_set, 1)

            sort_key(0)

            sort_key(1)
            dve.wait_ge(rec_in[0], 16)

            def radial_basis(g, q, b):
                dve.wait_ge(tanh_done, g + 1)
                V.tensor_scalar(up1, th[b], 1.0, None, ALU.add).then_inc(rbf_chain, 1)
                dve.wait_ge(rbf_chain, 2 * g + 1)
                if not (isinstance(g, int) and g == 0):
                    dve.wait_ge(rbf_done, g)
                V.reciprocal(rcp, up1).then_inc(rbf_chain, 1)
                dve.wait_ge(rbf_chain, 2 * g + 2)
                if not (isinstance(g, int) and g < 2):
                    dve.wait_ge(l1_mm, g - 1)
                V.scalar_tensor_tensor(rbf[b], rcp, -0.5, de[b][:, 1, :], ALU.add, ALU.mult).then_inc(rbf_done, 1)

            def one_hot(k, g, b, s):
                V.tensor_tensor(hot[b][:, :, :], lane[:, None, :].to_broadcast([P, GT, P]),
                                rec[k][:, bass.ds(g * GT, GT), 0:1].to_broadcast([P, GT, P]),
                                ALU.is_equal).then_inc(s, 1)

            def messages(g, q, b):
                dve.wait_ge(gathered[b], 16 * GT * q + 16 * GT)
                for h in range(2):
                    dve.wait_ge(l5_mm, 2 * g + h + 1)
                    V.tensor_tensor(msg[:, 2 * h:2 * h + 2, :].rearrange("p a b -> p (a b)"), ps[:, 5 + h, :],
                                    gath[b][:, 2 * h:2 * h + 2, :].rearrange("p a b -> p (a b)"),
                                    ALU.mult).then_inc(msg_done, 1)

            def blocks_of(k, g):
                return nc.values_load_multi_w_load_instructions(
                    block_of[k][0:1, bass.ds(g * GT, GT)], [mybir.EngineType.DVE], min_val=0, max_val=NB - 1,
                    skip_runtime_bounds_check_because="a count of at most NB block starts, less one, and the "
                                                      "first block starts at tile 0")[1]

            def add_up(g):
                blocks = blocks_of(0, g)
                for t in range(GT):
                    if not (isinstance(g, int) and g == 0 and t == 0):
                        dve.wait_ge(added, GT * g + t)
                    dve.wait_ge(agg_mm, 2 * g + t // 2 + 1)
                    rows_of = agg[:, bass.ds(blocks[t] * H, H)]
                    V.tensor_tensor(rows_of, rows_of, ps[:, 7 * (1 - t // 2), (t % 2) * H:(t % 2 + 1) * H],
                                    ALU.add).then_inc(added, 1)

            def dve_group(ahead=True, before_it=True):
                def body(g, q, b):
                    if ahead:
                        radial_basis(g + 2, q + 1, b)
                    one_hot(0, g, b, hot_done)
                    if before_it:
                        messages(g - 1, q + b - 1, 1 - b)
                        add_up(g - 1)
                return body

            radial_basis(0, 0, 0)
            radial_basis(1, 0, 1)
            single(dve_group(before_it=False), 0)
            single(dve_group(), 1, 2)
            pairs(dve, dve_group(), 3, 204)
            single(dve_group(), 205)
            single(dve_group(ahead=False), 206, 207)
            messages(207, 103, 1)
            add_up(207)

            for k in range(2):
                V.memset(msg2[k][:, :, HALF:ACW], 1.0)
            for b in range(2):
                dve.wait_ge(scattered[1][b], 16 * GT * (SGROUPS // 2))

            def by_block(t):
                return t.rearrange("p (j n) -> p j n", j=CB)

            def moments(step, src):
                for j in range(CB):
                    last = V.bn_stats(stats[:, j, :], by_block(src)[:, j, :])
                step(last)
                dve.sem_inc(carrier)
                for j in range(CB):
                    last = V.bn_aggr(mv[:, j, :], stats[:, j, :])
                step(last)
                step(V.tensor_scalar(var_eps[:, :], mv[:, :, 1], EPS_LN, None, ALU.add))

            def normalise(step, dst, src):
                step(V.reciprocal(rstd[:, :], std[:, :]))
                for j in range(CB):
                    last = V.tensor_scalar(by_block(dst)[:, j, :], by_block(src)[:, j, :], mv[:, j, 0:1],
                                           rstd[:, j:j + 1], ALU.subtract, ALU.mult)
                step(last)

            def node_chunk(c):
                step = stepper(nv, NV * c)
                dve.wait_ge(x_in, 16 * c + 16)
                step(V.tensor_tensor(chunk[1], chunk[0], agg[:, bass.ds(c * (CB * H), CB * H)], ALU.add))
                moments(step, chunk[1])
                assert step.count[0] == NV_VAR1
                dve.wait_ge(nact, NACT * c + NACT_STD)
                normalise(step, chunk[2], chunk[1])
                step(V.tensor_tensor(by_block(chunk[2]), by_block(chunk[2]), gb[:, 0:1, :].to_broadcast([P, CB, H]), ALU.mult))
                step(V.tensor_tensor(by_block(chunk[2]), by_block(chunk[2]), gb[:, 1:2, :].to_broadcast([P, CB, H]), ALU.add))
                assert step.count[0] == NV_OUT
                dve.wait_ge(nact, NACT * c + NACT_GATE)
                step(V.scalar_tensor_tensor(chunk[6], chunk[4], 1.0, chunk[2], ALU.add, ALU.mult))
                step(V.scalar_tensor_tensor(chunk[1], chunk[6], 0.5, chunk[0], ALU.mult, ALU.add))
                moments(step, chunk[1])
                assert step.count[0] == NV_VAR2
                dve.wait_ge(nact, NACT * c + NACT_STD2)
                if not isinstance(c, int):
                    dve.wait_ge(x1_out, 32 * c)
                    dve.wait_ge(nact, NACT * c)
                normalise(step, chunk[5], chunk[1])
                assert step.count[0] == NV

            chunks(dve, node_chunk)
            dve.wait_ge(x1_out, 32 * CHUNKS)
            dve.wait_ge(nact, NACT * CHUNKS)
            V.memset(arena1[:, 0:2 * NB * ACW], 0.0)
            dve.wait_ge(rec_in[1], 16)

            for k in range(2):
                def scale(g, q, b):
                    dve.wait_ge(gathered2[b], 16 * GT * (q + 1 + GROUPS // 2 * k))
                    V.tensor_tensor(msg2[b][:, :, 0:HALF], gath[b][:, :, 0:HALF],
                                    rec[k][:, bass.ds(g * GT, GT), 2:3].to_broadcast([P, GT, HALF]),
                                    ALU.mult).then_inc(scaled, 1)

                def sums(g, b):
                    blocks = blocks_of(k, g)
                    for t in range(GT):
                        n = GT * g + t + GT * GROUPS * k
                        if not (isinstance(n, int) and n == 0):
                            dve.wait_ge(added2, n)
                        dve.wait_ge(agg2_mm, 2 * g + t // 2 + 1 + 2 * GROUPS * k)
                        rows_of = acc[k][:, bass.ds(blocks[t] * ACW, ACW)]
                        V.tensor_tensor(rows_of, rows_of,
                                        ps[:, 2 * b + t // 2, (t % 2) * H:(t % 2) * H + ACW],
                                        ALU.add).then_inc(added2, 1)

                def group2(g, q, b):
                    one_hot(k, g, b, hot2_done)
                    scale(g, q, b)
                    if not (isinstance(g, int) and g == 0):
                        sums(g - 1, 1 - b)

                single(group2, 0, 1, 2)
                pairs(dve, group2, 3, 204)
                single(group2, 205, 206, 207)
                sums(207, 1)

            step = stepper(chain, step.count[0])
            step.count[0] = 0
            for k in range(2):
                deg = acc[k].rearrange("p (n f) -> p n f", f=ACW)[:, :, HALF]
                step(V.tensor_scalar(rdeg[k][:, :], deg, 1.0, None, ALU.max))
                step(V.reciprocal(rdeg[k][:, :], rdeg[k][:, :]))

            def last_chunk(c):
                step = stepper(fv, FV * c)
                for k in range(2):
                    sums_of = acc[k][:, bass.ds(c * (CB * ACW), CB * ACW)].rearrange("p (j f) -> p j f", f=ACW)
                    last = V.tensor_tensor(by_block(last_c[1])[:, :, k * HALF:(k + 1) * HALF], sums_of[:, :, 0:HALF],
                                           rdeg[k][:, bass.ds(c * CB, CB), None].to_broadcast([P, CB, HALF]),
                                           ALU.mult)
                step(last)
                step(V.tensor_tensor(last_c[0], last_c[1], agg[:, bass.ds(c * (CB * H), CB * H)], ALU.add))
                moments(step, last_c[0])
                assert step.count[0] == FV_VAR
                dve.wait_ge(fact, c + 1)
                if not isinstance(c, int):
                    dve.wait_ge(out_done, 16 * c)
                normalise(step, last_c[2], last_c[0])
                assert step.count[0] == FV

            chunks(dve, last_chunk)


def kernel(x, src, dst, edge_weight, L0_gnn_centers, L0_gnn_widths, L0_gnn_rbf_w1, L0_gnn_rbf_b1,
           L0_gnn_rbf_w2, L0_gnn_rbf_b2, L0_gnn_filt_w1, L0_gnn_filt_b1, L0_gnn_filt_w2, L0_gnn_filt_b2,
           L0_gnn_filt_w3, L0_gnn_filt_b3, L0_gnn_node_w, L0_gnn_node_b, L0_gnn_ln_g, L0_gnn_ln_b,
           L0_gnn_gate_w, L0_gnn_gate_b):
    import numpy as np
    import concourse.bacc as bacc
    from concourse.bass_utils import run_bass_kernel_spmd

    def arr(a):
        return np.ascontiguousarray(np.asarray(a))

    def edges(a, pad):
        a = np.asarray(a)
        return np.concatenate([a, np.full(P * EC - E, pad, a.dtype)]).reshape(P, EC)

    xp = np.concatenate([np.asarray(x), np.zeros((NP - N, H), np.float32)])
    twice = lambda a: np.tile(np.asarray(a), 2)
    f_b1, f_b2 = np.asarray(L0_gnn_filt_b1), np.asarray(L0_gnn_filt_b2)
    cols = np.stack([twice(L0_gnn_centers), twice(L0_gnn_widths), twice(L0_gnn_rbf_b1), f_b1[:P], f_b1[P:],
                     f_b2[:P], f_b2[P:], twice(L0_gnn_rbf_b2)], axis=1)
    rows = np.tile(np.concatenate([np.asarray(a) for a in (L0_gnn_filt_b3, L0_gnn_node_b, L0_gnn_gate_b)]), (3, 1))
    arrays = {
        "x": xp, "xT": arr(xp.T),
        "src": edges(src, PAD_NODE), "dst": edges(dst, PAD_NODE), "wgt": edges(edge_weight, 0.0),
        "cols": arr(cols), "rows": arr(rows), "ln_gb": np.stack([np.asarray(L0_gnn_ln_g), np.asarray(L0_gnn_ln_b)]),
        "w1": arr(L0_gnn_rbf_w1), "w2T": arr(np.tile(np.asarray(L0_gnn_rbf_w2).T, (1, 2))),
        "f1": arr(L0_gnn_filt_w1), "f2": arr(L0_gnn_filt_w2), "f3": arr(L0_gnn_filt_w3),
        "node_w": arr(L0_gnn_node_w), "gate_w": arr(L0_gnn_gate_w),
    }
    nc = bacc.Bacc("TRN2", target_bir_lowering=False, num_devices=1)
    args = [nc.dram_tensor(k, a.shape, mybir.dt.from_np(a.dtype), kind="ExternalInput").ap()
            for k, a in arrays.items()]
    out = nc.dram_tensor("out", (NP, H), mybir.dt.float32, kind="ExternalOutput").ap()
    build(nc, *args, out)
    result = run_bass_kernel_spmd(nc, [arrays], core_ids=[0])
    return result.results[0]["out"][:N]
```

```python
import math
from contextlib import ExitStack

import concourse.bass as bass
import concourse.mybir as mybir

P = 128
N = 6250
H = 256
HALF = H // 2
R = 64
NB = -(-N // P)
NP = NB * P
E = 100000
GT = 4
SU = 6
EC = -(-E // (P * SU)) * SU
CA = EC * 11 // 30 // (2 * SU) * 2 * SU
COLS = (CA, EC - CA, EC)
COL0 = (0, CA, 0)
UNITS = tuple(n // SU for n in COLS)
ST = tuple(-(-((P * n + NB * (P - 1)) // P) // GT) * GT for n in COLS)
TILE0 = (0, ST[0], 0)
TILES = (ST[0] + ST[1], ST[2])
GROUPS = tuple(t // GT for t in TILES)
G0, G1 = GROUPS
GA = ST[0] // GT
GB = UNITS[1] - 2
GR = 3
NB2 = NB + NB % 2
assert UNITS[0] % 2 == 0 and GA % 2 == 0 and GB % 2 == 1 and GB + 1 < GA and GA + UNITS[2] < G0
assert G0 % 2 == 1 and G1 % 2 == 1 and GR + NB < GA and NB % 2 == 1
PAD_NODE = NP - 1
CB = 7
CHUNKS = NB // CB
ACW = HALF + 1
GW = GT * P // 2
CUTOFF = 10.0
EPS_W = 1e-5
EPS_LN = 1e-5
NV_VAR1, NV_OUT, NV_VAR2, NV = 4, 8, 13, 15
NPE = 8
NACT_STD, NACT_T, NACT_GATE, NACT_STD2, NACT = 1, 5, 9, 10, 11
FV_VAR, FV = 5, 7
ROUND = 1.5 * 2.0 ** 23


def build(nc, x, xT, src, dst, wgt, cols, rows, ln_gb, w1, w2T, f1, f2, f3, node_w, gate_w, out):
    f32, bf16, i32 = mybir.dt.float32, mybir.dt.bfloat16, mybir.dt.int32
    ALU, ACT = mybir.AluOpType, mybir.ActivationFunctionType

    y_rows = nc.dram_tensor("y_rows", (NP, H), f32).ap()
    x1_half = [nc.dram_tensor(f"x1_half{k}", (NP, HALF), f32).ap() for k in range(2)]
    records = [nc.dram_tensor(f"records{s}", (P * ST[s], 4), f32).ap() for s in range(3)]
    slot_rows = nc.dram_tensor("slot_rows", (2, TILES[0] * P), f32).ap()

    with ExitStack() as ctx:
        def sb(name, shape, dt=f32):
            return ctx.enter_context(nc.sbuf_tensor(name, shape, dt))

        def sem(name):
            return ctx.enter_context(nc.semaphore(name))

        lane = sb("lane", [P, P])
        ident = sb("ident", [P, P])
        before = sb("before", [P, P])
        ones = sb("ones", [P, P])
        ones3 = sb("ones3", [3, P], bf16)
        w1d = sb("w1d", [P, P])
        w2t = sb("w2t", [R, P])
        f1s = sb("f1s", [R, H])
        w23 = sb("w23", [P, H])
        f2s = sb("f2s", [P, 2, H])
        f3s = sb("f3s", [P, 2, H])
        nws = sb("nws", [P, 2, H])
        gws = sb("gws", [P, 2, H])
        gb = sb("gb", [P, 2, H])
        col = sb("col", [P, 8])
        negc = sb("negc", [P, 1])
        zscale = sb("zscale", [P, 1])
        b23 = sb("b23", [P, 2])
        r3 = sb("r3", [3, 3 * H])
        r3b = [sb(f"r3b{k}", [3, 3 * H]) for k in range(2)]
        part = [sb(f"part{k}", [3, 3 * H], bf16) for k in range(3)]
        bias3 = sb("bias3", [3, 3, H], bf16)

        agg = sb("agg", [P, NB * H])
        rec = [sb(f"rec{k}", [P, TILES[k], 4]) for k in range(2)]
        table = sb("table", [P, TILES[0]], i32)
        TROW = (0, 32, 64)
        cnt = sb("cnt", [P, NB2])
        tot = sb("tot", [P, NB])
        start = sb("start", [P, NB])
        nt_i = sb("nt_i", [P, NB], i32)
        offs = sb("offs", [P, NB2])
        ntc = sb("ntc", [NB, 1])
        ntc_i = sb("ntc_i", [NB, 1], i32)
        startc = sb("startc", [NB, 1])

        A1 = 17 * EC
        arena1 = sb("arena1", [P, A1])
        at = 0

        def take(n):
            nonlocal at
            at += n
            return arena1[:, at - n:at]

        stage_rec = [take(4 * EC) for _ in range(2)]
        stage_adr = [take(EC).bitcast(i32) for _ in range(2)]
        key_i = [take(EC).bitcast(i32) for _ in range(2)]
        wt = take(EC)
        blk, eq, run, rank = take(EC), take(EC), take(EC), take(EC)
        acc = [arena1[:, k * NB * ACW:(k + 1) * NB * ACW] for k in range(2)]

        chunk = [arena1[:, k * CB * H:(k + 1) * CB * H] for k in range(7)]

        arena2 = sb("arena2", [P, 33 * GW])
        at2 = 0

        def ring(*shape):
            nonlocal at2
            n = math.prod(shape)
            v = arena2[:, at2:at2 + n]
            at2 += n
            if len(shape) == 2:
                v = v.rearrange("p (a b) -> p a b", a=shape[0])
            if len(shape) == 3:
                v = v.rearrange("p (a b c) -> p a b c", a=shape[0], b=shape[1])
            return v

        gath = [ring(GT, H) for _ in range(2)]
        de = [ring(2, GW) for _ in range(2)]
        sq = ring(GW)
        th = [ring(GW) for _ in range(2)]
        up1 = ring(GW)
        rcp = ring(GW)
        rbf = [ring(GW) for _ in range(2)]
        s1 = [ring(GW) for _ in range(2)]
        s2 = ring(2, GT * P)
        s3 = ring(2, GT * P)
        msg = ring(GT, H)
        assert at2 == 33 * GW and 17 * EC >= 7 * CB * H
        last_c = [arena2[:, k * CB * H:(k + 1) * CB * H] for k in range(3)]
        xt_c = last_c[0].rearrange("p (k n) -> p k n", k=2)
        y_c = last_c[1].rearrange("p (j n) -> p j n", j=CB)
        tile_no = arena2[:, 2 * CB * H:2 * CB * H + TILES[0]]
        reached = arena2[0:NB, 2 * CB * H + TILES[0]:2 * CB * H + 2 * TILES[0]]
        at2 = 2 * CB * H + 2 * TILES[0]
        eq1, run1, rank1 = ring(COLS[1]), ring(COLS[1]), ring(COLS[1])
        assert at2 <= 33 * GW
        RB = -(-max(ST[0], ST[1]) // P)
        rows_of_slots = sb("rows_of_slots", [P, 2, RB, P])
        msg2 = [(s2, s3)[k].rearrange("p a b -> p (a b)")[:, 0:GT * ACW].rearrange("p (t f) -> p t f", t=GT)
                for k in range(2)]
        hot = [sb(f"hot{k}", [P, GT, P]) for k in range(2)]
        idx = [sb(f"idx{k}", [P, GT], i32) for k in range(2)]
        sc_rec = [sb(f"sc_rec{k}", [P, SU, 4]) for k in range(2)]
        sc_adr = [sb(f"sc_adr{k}", [P, SU], i32) for k in range(2)]
        stats = sb("stats", [P, CB, 6])
        mv = sb("mv", [P, CB, 2])
        var_eps = sb("var_eps", [P, CB])
        std = sb("std", [P, CB])
        rstd = sb("rstd", [P, CB])
        rdeg = [sb(f"rdeg{k}", [P, NB]) for k in range(2)]

        ps = ctx.enter_context(nc.psum_tensor("ps", [P, 8, 512], f32))

        edges_in, weights_in = sem("edges_in"), sem("weights_in")
        default_set, default_out = sem("default_set"), sem("default_out")
        consts = sem("consts")
        carrier = sem("carrier")
        fused_mm, params_set, biases_set = sem("fused_mm"), sem("params_set"), sem("biases_set")
        counted, prefix_mm, tiles_set = sem("counted"), sem("prefix_mm"), sem("tiles_set")
        starts_mm, reached_set, table_mm, table_set = (
            sem("starts_mm"), sem("reached_set"), sem("table_mm"), sem("table_set"))
        envelope = sem("envelope")
        chain = sem("chain")
        sorted_key = sem("sorted_key")
        xt_in, y_mm, y_evac, y_out = sem("xt_in"), sem("y_mm"), sem("y_evac"), sem("y_out")
        sc_staged = sem("sc_staged")
        scattered = [[sem(f"scattered{k}{b}") for b in range(2)] for k in range(3)]
        rec_in = [sem(f"rec_in{s}") for s in range(3)]
        rank_chain = sem("rank_chain")
        rows_mm, rows_evac, rows_out = sem("rows_mm"), sem("rows_evac"), sem("rows_out")
        de_in = [sem(f"de_in{b}") for b in range(2)]
        squared, tanh_done, rbf_done = sem("squared"), sem("tanh_done"), sem("rbf_done")
        rbf_chain = sem("rbf_chain")
        l1_mm, l23_mm, l4_mm, l5_mm = sem("l1_mm"), sem("l23_mm"), sem("l4_mm"), sem("l5_mm")
        s1_done, s2_done, s3_done = sem("s1_done"), sem("s2_done"), sem("s3_done")
        idx_staged = sem("idx_staged")
        gathered = [sem(f"gathered{b}") for b in range(2)]
        hot_done, msg_done, agg_mm, added = sem("hot_done"), sem("msg_done"), sem("agg_mm"), sem("added")
        x_in, nv, npe, nact, x1_out = sem("x_in"), sem("nv"), sem("npe"), sem("nact"), sem("x1_out")
        idx2_staged = [sem(f"idx2_staged{k}") for k in range(2)]
        gathered2 = [[sem(f"gathered2{k}{b}") for b in range(2)] for k in range(2)]
        hot2_done = [sem(f"hot2_done{k}") for k in range(2)]
        scaled = [sem(f"scaled{k}") for k in range(2)]
        agg2_mm = [sem(f"agg2_mm{k}") for k in range(2)]
        added2 = [sem(f"added2{k}") for k in range(2)]
        fv, fact, out_done = sem("fv"), sem("fact"), sem("out_done")

        block = ctx.enter_context(nc.Block())

        y_v = y_rows.rearrange("(c j p) n -> c p j n", p=P, j=CB)
        x_v = x.rearrange("(c j p) n -> c p j n", p=P, j=CB)
        out_v = out.rearrange("(c j p) n -> c p j n", p=P, j=CB)
        x1_v = [t.rearrange("(c j p) n -> c p j n", p=P, j=CB) for t in x1_half]
        xT_v = xT.rearrange("(k p) (c n) -> c p k n", p=P, c=CHUNKS)
        rec_v = [t.rearrange("(p t) f -> p t f", p=P) for t in records]

        def hold(eng, s, value):
            eng.wait_ge(s, value)
            eng.sem_inc(carrier)

        def pairs(eng, body, lo, hi):
            with eng.Fori((lo + 1) // 2, hi // 2 + 1) as i:
                body(2 * i - 1, i - 1, 1)
                body(2 * i, i, 0)

        def chunks(eng, body):
            body(0)
            with eng.Fori(1, CHUNKS) as c:
                body(c)

        def single(body, *groups):
            for g in groups:
                body(g, g // 2, g % 2)

        def all_groups(eng, body, n):
            single(body, 0, 1, 2)
            pairs(eng, body, 3, n - 3)
            single(body, n - 2, n - 1)

        def slot_uses(n, b):
            return (n + 1 - b) // 2

        def table_parts(s):
            n = -(-ST[s] // 512)
            cuts = [ST[s] * i // n for i in range(n + 1)]
            return [(5 + 2 * i, cuts[i], cuts[i + 1]) for i in range(n)]

        def row_blocks(s):
            for f in range(2):
                for j in range(-(-ST[s] // P)):
                    bank, c = (5 + f, j * P) if j < 4 else (7, f * P)
                    yield f, j, min(P, ST[s] - j * P), bank, c

        n_weights = 12

        @block.sync
        def _(sp):
            for t, d in ((key_i[0], src), (key_i[1], dst), (wt, wgt)):
                sp.dma_start(t, d).then_inc(edges_in, 16)
            for t, d in ((w2t, w2T), (f1s, f1), (col, cols), (r3, rows)):
                sp.dma_start(t[:, :], d).then_inc(weights_in, 16)
            for t, d in ((f2s, f2), (f3s, f3), (nws, node_w), (gws, gate_w)):
                sp.dma_start(t[:, :, :], d.rearrange("(k p) n -> p k n", p=P)).then_inc(weights_in, 16)
            for k in range(2):
                sp.dma_start(gb[:, k, :], ln_gb[k:k + 1, :].to_broadcast([P, H])).then_inc(weights_in, 16)
            sp.wait_ge(default_set, 5)
            for h in range(2):
                sp.dma_start(w1d[h * R:(h + 1) * R, h * R:(h + 1) * R], w1).then_inc(weights_in, 16)
            for s in range(3):
                sp.dma_start(rec_v[s], rec[0][:, 0:ST[s], :]).then_inc(default_out, 16)

            def y_step(c):
                sp.dma_start(xt_c, xT_v[c]).then_inc(xt_in, 16)
                sp.wait_ge(y_evac, 4 * c + 4)
                sp.dma_start(y_v[c], y_c).then_inc(y_out, 16)

            with sp.Fori(0, CHUNKS) as c:
                y_step(c)
            sp.wait_ge(y_out, 16 * CHUNKS)

            def load_part(s):
                for b in range(2):
                    sp.wait_ge(scattered[s][b], 16 * SU * slot_uses(UNITS[s], b))
                sp.dma_start(rec[0][:, TILE0[s]:TILE0[s] + ST[s], :], rec_v[s]).then_inc(rec_in[s], 16)
                sp.wait_ge(rows_evac, 4 * s + 4)
                full = ST[s] // P
                for f in range(2):
                    o = slot_rows[f, TILE0[s] * P:(TILE0[s] + ST[s]) * P]
                    sp.dma_start(o[0:full * P * P].rearrange("(j t l) -> t j l", t=P, l=P),
                                 rows_of_slots[:, f, 0:full, :]).then_inc(rows_out, 16)
                    sp.dma_start(o[full * P * P:ST[s] * P].rearrange("(t l) -> t l", l=P),
                                 rows_of_slots[0:ST[s] - full * P, f, full, :]).then_inc(rows_out, 16)
                sp.wait_ge(rows_out, 64 * s + 64)

            load_part(0)

            def load_de(g, q, b):
                if not (isinstance(g, int) and g < 2):
                    sp.wait_ge(rbf_done, g - 1)
                for f in range(2):
                    for h in range(2):
                        sp.dma_start(de[b][h * R:(h + 1) * R, f, :],
                                     slot_rows[f:f + 1, bass.ds(g * (GT * P) + h * GW, GW)].to_broadcast([R, GW])
                                     ).then_inc(de_in[b], 16)

            single(load_de, 0, 1, 2)
            pairs(sp, load_de, 3, GA - 2)
            single(load_de, GA - 1)
            load_part(1)
            single(load_de, GA)
            pairs(sp, load_de, GA + 1, G0 - 1)

            for b in range(2):
                sp.wait_ge(scattered[2][b], 16 * SU * slot_uses(UNITS[2], b))
            sp.dma_start(rec[1][:, :, :], rec_v[2]).then_inc(rec_in[2], 16)

            with sp.Fori(0, CHUNKS) as c:
                sp.dma_start(chunk[0].rearrange("p (j n) -> p j n", j=CB), x_v[c]).then_inc(x_in, 16)
                sp.wait_ge(nv, NV * c + NV)
                for k in range(2):
                    sp.dma_start(x1_v[k][c], chunk[5].rearrange("p (j n) -> p j n", j=CB)
                                 [:, :, k * HALF:(k + 1) * HALF]).then_inc(x1_out, 16)

            with sp.Fori(0, CHUNKS) as c:
                sp.wait_ge(fv, FV * c + FV)
                sp.dma_start(out_v[c], last_c[2].rearrange("p (j n) -> p j n", j=CB)).then_inc(out_done, 16)
            sp.wait_ge(out_done, 16 * CHUNKS)

        @block.gpsimd
        def _(pool):
            nc.gpsimd.iota(lane[:, :], [[1, P]], base=0, channel_multiplier=0,
                           allow_small_or_imprecise_dtypes=True).then_inc(consts, 1)
            nc.gpsimd.iota(tile_no, [[1, TILES[0]]], base=0, channel_multiplier=0,
                           allow_small_or_imprecise_dtypes=True).then_inc(consts, 1)
            nc.gpsimd.memset(ones[:, :], 1.0).then_inc(consts, 1)
            nc.gpsimd.memset(ones3[:, :], 1.0).then_inc(consts, 1)
            pool.wait_ge(consts, 4)
            nc.gpsimd.affine_select(out=before[:, :], in_=ones[:, :], compare_op=ALU.is_gt, fill=0.0,
                                    base=0, pattern=[[1, P]], channel_multiplier=-1).then_inc(consts, 1)
            nc.gpsimd.affine_select(out=ident[:, :], in_=ones[:, :], compare_op=ALU.is_equal, fill=0.0,
                                    base=0, pattern=[[1, P]], channel_multiplier=-1).then_inc(consts, 1)

            nc.gpsimd.memset(agg[:, :], 0.0).then_inc(consts, 1)

            def scatter(s):
                def body(u, q, b):
                    hold(pool, sc_staged, 2 * u + 2 + 2 * sum(UNITS[:s]))
                    for t in range(SU):
                        pool.indirect_dma_start(
                            records[s], bass.IndirectOffsetOnAxis(ap=sc_adr[b][:, t:t + 1], axis=0),
                            sc_rec[b][:, t, :], None).then_inc(scattered[s][b], 16)
                return body

            def gather(g, q, b):
                hold(pool, idx_staged, g + 1)
                if not (isinstance(g, int) and g < 2):
                    hold(pool, msg_done, 2 * g - 2)
                for t in range(GT):
                    pool.indirect_dma_start(
                        gath[b][:, t, :], None, y_rows,
                        bass.IndirectOffsetOnAxis(ap=idx[b][:, t:t + 1], axis=0)).then_inc(gathered[b], 16)

            pool.wait_ge(default_out, 48)
            single(scatter(0), 0, 1, 2)
            pairs(pool, scatter(0), 3, UNITS[0] - 2)
            single(scatter(0), UNITS[0] - 1)
            single(scatter(1), 0, 1)

            def gather_scatter_src(g, q, b):
                gather(g, q, b)
                scatter(1)(g + 2, q + 1, b)

            def gather_scatter_dst(g, q, b):
                gather(g, q, b)
                scatter(2)(g - GA, q - GA // 2, b)

            pool.wait_ge(y_out, 16 * CHUNKS)
            single(gather_scatter_src, 0, 1, 2)
            pairs(pool, gather_scatter_src, 3, GB - 1)
            single(gather, *range(GB, GA))
            single(gather_scatter_dst, GA, GA + 1, GA + 2)
            pairs(pool, gather_scatter_dst, GA + 3, GA + UNITS[2] - 1)
            single(gather, GA + UNITS[2], GA + UNITS[2] + 1)
            pairs(pool, gather, GA + UNITS[2] + 2, G0 - 3)
            single(gather, G0 - 2, G0 - 1)

            pool.wait_ge(x1_out, 32 * CHUNKS)
            for k in range(2):
                def gather2(g, q, b):
                    hold(pool, idx2_staged[k], g + 1)
                    if not (isinstance(g, int) and g < 2):
                        hold(pool, scaled[k], g - 1)
                    for t in range(GT):
                        pool.indirect_dma_start(
                            gath[b][:, t, 0:HALF], None, x1_half[k],
                            bass.IndirectOffsetOnAxis(ap=idx[b][:, t:t + 1], axis=0)).then_inc(gathered2[k][b], 16)
                if k:
                    hold(pool, scaled[0], G0)
                all_groups(pool, gather2, GROUPS[k])

        @block.scalar
        def _(act):
            act.wait_ge(envelope, 1)
            nc.scalar.activation(run, eq, ACT.Sin).then_inc(envelope, 1)

            def y_evacuate(c):
                if not isinstance(c, int):
                    act.wait_ge(y_out, 16 * c)
                for j in range(4):
                    w = 2 if j < 3 else 1
                    act.wait_ge(y_mm, 4 * c + j + 1)
                    nc.scalar.activation(y_c[:, 2 * j:2 * j + w, :].rearrange("p a b -> p (a b)"),
                                         ps[:, j, 0:w * H], ACT.Copy).then_inc(y_evac, 1)

            chunks(act, y_evacuate)

            def stage(s):
                def body(u, q, b):
                    if not isinstance(u, int) or u >= 2:
                        hold(act, scattered[s][b], 16 * SU * q)
                    elif s:
                        hold(act, scattered[s - 1][b], 16 * SU * slot_uses(UNITS[s - 1], b))
                    nc.scalar.activation(sc_rec[b][:, :, :].rearrange("p a b -> p (a b)"),
                                         stage_rec[s // 2][:, bass.ds(u * (4 * SU) + 4 * COL0[s], 4 * SU)],
                                         ACT.Copy).then_inc(sc_staged, 1)
                    nc.scalar.activation(sc_adr[b][:, :], stage_adr[s // 2][:, bass.ds(u * SU + COL0[s], SU)],
                                         ACT.Copy).then_inc(sc_staged, 1)
                return body

            act.wait_ge(sorted_key, 1)
            single(stage(0), 0, 1, 2)
            pairs(act, stage(0), 3, UNITS[0] - 2)
            single(stage(0), UNITS[0] - 1)
            act.wait_ge(sorted_key, 2)
            single(stage(1), 0, 1)

            def evacuate_rows(s):
                act.wait_ge(rows_mm, s + 1)
                if s:
                    act.wait_ge(rows_out, 64)
                full = ST[s] // P
                for f, j, w, bank, c in row_blocks(s):
                    if j == full - 1:
                        nc.scalar.activation(rows_of_slots[:, f, 0:full, :].rearrange("p a b -> p (a b)"),
                                             ps[:, bank, 0:full * P], ACT.Copy).then_inc(rows_evac, 1)
                    if j == full:
                        nc.scalar.activation(rows_of_slots[0:w, f, j, :], ps[0:w, bank, c:c + P],
                                             ACT.Copy).then_inc(rows_evac, 1)

            act.wait_ge(table_set, 3)
            evacuate_rows(0)

            def radial(g, q, b):
                act.wait_ge(de_in[b], 64 * q + 64)
                if not (isinstance(g, int) and g == 0):
                    act.wait_ge(tanh_done, g)
                nc.scalar.activation(sq, de[b][:, 0, :], ACT.Square, bias=negc[:, 0:1]).then_inc(squared, 1)
                act.wait_ge(squared, g + 1)
                nc.scalar.activation(th[b], sq, ACT.Tanh, scale=zscale[:, 0:1]).then_inc(tanh_done, 1)

            def silu1(g, q, b):
                act.wait_ge(l1_mm, g + 1)
                nc.scalar.activation(s1[b], ps[:, 0, 0:GW], ACT.Silu,
                                     bias=col[:, 2:3]).then_inc(s1_done, 1)

            def silu2(g):
                act.wait_ge(l23_mm, g + 1)
                for m in range(2):
                    nc.scalar.activation(s2[:, m, :].rearrange("p (h e) -> p h e", h=2),
                                         ps[:, 1:3, m * GW:(m + 1) * GW], ACT.Silu,
                                         bias=b23[:, m:m + 1]).then_inc(s2_done, 1)

            def silu3(g):
                for m in range(2):
                    act.wait_ge(l4_mm, 2 * g + m + 1)
                    nc.scalar.activation(s3[:, m, :], ps[:, 3 + m, :], ACT.Silu,
                                         bias=col[:, 5 + m:6 + m]).then_inc(s3_done, 1)

            def stage_idx(g, q, b):
                if not (isinstance(g, int) and g < 2):
                    hold(act, gathered[b], 16 * GT * q)
                nc.scalar.activation(idx[b][:, :], rec[0][:, bass.ds(g * GT, GT), 1],
                                     ACT.Copy).then_inc(idx_staged, 1)

            def act_group(scatters, ahead=2):
                def body(g, q, b):
                    silu2(g)
                    if ahead == 2:
                        radial(g + 2, q + 1, b)
                    if ahead:
                        stage_idx(g + 1, q + b, 1 - b)
                    if scatters == 1:
                        stage(1)(g + 2, q + 1, b)
                    if scatters == 2:
                        stage(2)(g - GA, q - GA // 2, b)
                    silu3(g)
                    if ahead:
                        silu1(g + 1, q + b, 1 - b)
                return body

            act.wait_ge(weights_in, 16 * n_weights)
            act.wait_ge(params_set, 2)
            act.wait_ge(rec_in[0], 16)
            radial(0, 0, 0)
            radial(1, 0, 1)
            stage_idx(0, 0, 0)
            silu1(0, 0, 0)
            single(act_group(1), 0, 1, 2)
            pairs(act, act_group(1), 3, GB - 1)
            single(act_group(0), GB)
            evacuate_rows(1)
            act.wait_ge(rec_in[1], 16)
            single(act_group(0), *range(GB + 1, GA))
            act.wait_ge(sorted_key, 3)
            single(act_group(2), GA, GA + 1, GA + 2)
            pairs(act, act_group(2), GA + 3, GA + UNITS[2] - 1)
            single(act_group(0), GA + UNITS[2], GA + UNITS[2] + 1)
            pairs(act, act_group(0), GA + UNITS[2] + 2, G0 - 3)
            single(act_group(0, 1), G0 - 2)
            single(act_group(0, 0), G0 - 1)

            with act.Fori(0, CHUNKS) as c:
                act.wait_ge(nv, NV * c + NV_VAR1)
                nc.scalar.activation(std[:, :], var_eps[:, :], ACT.Sqrt).then_inc(nact, 1)
                for j in range(4):
                    w = 4 * P if j < 3 else 2 * P
                    act.wait_ge(npe, NPE * c + j + 1)
                    nc.scalar.activation(chunk[3][:, j * 4 * P:j * 4 * P + w], ps[:, j, 0:w],
                                         ACT.Copy).then_inc(nact, 1)
                for j in range(4):
                    w = 2 * H if j < 3 else H
                    act.wait_ge(npe, NPE * c + 4 + j + 1)
                    nc.scalar.activation(chunk[4][:, j * 2 * H:j * 2 * H + w], ps[:, 4 + j, 0:w],
                                         ACT.Tanh, scale=0.5).then_inc(nact, 1)
                act.wait_ge(nv, NV * c + NV_VAR2)
                nc.scalar.activation(std[:, :], var_eps[:, :], ACT.Sqrt).then_inc(nact, 1)
                hold(act, nv, NV * c + NV)
                nc.scalar.activation(agg[:, bass.ds(c * (CB * H), CB * H)], chunk[5],
                                     ACT.Copy).then_inc(nact, 1)

            act.wait_ge(rec_in[2], 16)
            for k in range(2):
                def stage_idx2(g, q, b):
                    if not isinstance(g, int) or g >= 2:
                        hold(act, gathered2[k][b], 16 * GT * q)
                    elif k:
                        hold(act, gathered2[0][b], 16 * GT * slot_uses(G0, b))
                    nc.scalar.activation(idx[b][:, :], rec[k][:, bass.ds(g * GT, GT), 1],
                                         ACT.Copy).then_inc(idx2_staged[k], 1)
                all_groups(act, stage_idx2, GROUPS[k])

            with act.Fori(0, CHUNKS) as c:
                act.wait_ge(fv, FV * c + FV_VAR)
                nc.scalar.activation(std[:, :], var_eps[:, :], ACT.Sqrt).then_inc(fact, 1)

        @block.tensor
        def _(pe):
            mm = nc.tensor.matmul
            pe.wait_ge(weights_in, 16 * n_weights)
            pe.wait_ge(consts, 6)
            mm(ps[:, 4, 0:H], w2t[:, :], f1s[:, :], start=True, stop=True)
            for m in range(2):
                last = mm(ps[:, 5, m:m + 1], f1s[:, m * P:(m + 1) * P], col[0:R, 7:8], start=True, stop=True)
            last.then_inc(fused_mm, 1)
            pe.wait_ge(biases_set, 1)

            def y_product(c):
                pe.wait_ge(xt_in, 16 * c + 16)
                for j in range(CB):
                    if j % 2 == 0 and not isinstance(c, int):
                        pe.wait_ge(y_evac, 4 * c + j // 2 - 3)
                    o = ps[:, j // 2, (j % 2) * H:(j % 2 + 1) * H]
                    for k in range(2):
                        mm(o, xt_c[:, k, j * P:(j + 1) * P], nws[:, k, :], start=(k == 0), stop=False)
                    last = mm(o, ones3[:, :], bias3[:, 1, :], start=False, stop=True)
                    if j % 2 or j == CB - 1:
                        last.then_inc(y_mm, 1)

            def prefix(s):
                pe.wait_ge(counted, s + 1)
                mm(ps[:, 6, 0:NB], before[:, :], cnt[:, 0:NB], start=True, stop=True)
                mm(ps[:, 6, 64:64 + NB], ones[:, :], cnt[:, 0:NB], start=True, stop=True)
                mm(ps[0:NB, 6, 128:129], cnt[:, 0:NB], ones[:, 0:1], start=True, stop=True).then_inc(prefix_mm, 1)
                pe.wait_ge(tiles_set, s + 1)
                mm(ps[0:NB, 6, 130:131], before[0:NB, 0:NB], ntc[:, :], start=True, stop=True).then_inc(starts_mm, 1)
                pe.wait_ge(reached_set, s + 1)
                for bank, lo, hi in table_parts(s):
                    last = mm(ps[:, bank, 0:hi - lo], ones[0:NB, :], reached[:, lo:hi], start=True, stop=True)
                last.then_inc(table_mm, 1)
                pe.wait_ge(table_set, s + 1)

            y_product(0)
            with pe.Fori(1, 3) as c:
                y_product(c)
            prefix(0)
            with pe.Fori(3, CHUNKS) as c:
                y_product(c)
            prefix(1)
            prefix(2)

            def part_rows(s):
                pe.wait_ge(rec_in[s], 16)
                for f, j, w, bank, c in row_blocks(s):
                    at = TILE0[s] + j * P
                    last = nc.tensor.transpose(ps[0:w, bank, c:c + P], rec[0][:, at:at + w, 2 + f], ident[:, :])
                last.then_inc(rows_mm, 1)
                pe.wait_ge(rows_evac, 4 * s + 4)

            part_rows(0)

            def layer1(g, q, b):
                pe.wait_ge(rbf_done, g + 1)
                if not (isinstance(g, int) and g < 3):
                    pe.wait_ge(added, 4 * g - 8)
                mm(ps[:, 0, 0:GW], w1d[:, :], rbf[b], start=True, stop=True).then_inc(l1_mm, 1)

            def layer23(g, q, b):
                pe.wait_ge(s1_done, g + 1)
                for m in range(2):
                    for h in range(2):
                        last = mm(ps[:, 1 + h, m * GW:(m + 1) * GW],
                                  w23[h * R:(h + 1) * R, m * P:(m + 1) * P],
                                  s1[b][h * R:(h + 1) * R, :], start=True, stop=True)
                last.then_inc(l23_mm, 1)

            def layer4(g):
                pe.wait_ge(s2_done, 2 * g + 2)
                for m in range(2):
                    for k in range(2):
                        last = mm(ps[:, 3 + m, :], f2s[:, k, m * P:(m + 1) * P], s2[:, k, :],
                                  start=(k == 0), stop=(k == 1))
                    last.then_inc(l4_mm, 1)

            def layer5(g):
                pe.wait_ge(s3_done, 2 * g + 2)
                for t in range(GT):
                    if t % 2 == 0 and not (isinstance(g, int) and g < 1):
                        pe.wait_ge(msg_done, 2 * g + t // 2 - 1)
                    o = ps[:, 5 + t // 2, (t % 2) * H:(t % 2 + 1) * H]
                    for k in range(2):
                        mm(o, s3[:, k, t * P:(t + 1) * P], f3s[:, k, :], start=(k == 0), stop=False)
                    last = mm(o, ones3[:, :], bias3[:, 0, :], start=False, stop=True)
                    if t % 2:
                        last.then_inc(l5_mm, 1)

            def aggregate(g, b):
                pe.wait_ge(hot_done, g + 1)
                for h in range(2):
                    pe.wait_ge(msg_done, 2 * g + h + 1)
                    if not (isinstance(g, int) and g == 0):
                        pe.wait_ge(added, 4 * g - 2 + 2 * h)
                    if h:
                        pe.wait_ge(s1_done, min(g + 3, G0) if isinstance(g, int) else g + 3)
                    for t in (2 * h, 2 * h + 1):
                        last = mm(ps[:, 7 * (1 - h), (t % 2) * H:(t % 2 + 1) * H], hot[b][:, t, :], msg[:, t, :],
                                  start=True, stop=True)
                    last.then_inc(agg_mm, 1)

            def pe_group(g, q, b, before_it=True, after_it=True):
                layer23(g, q, b)
                if before_it:
                    layer5(g - 1)
                layer4(g)
                if after_it:
                    layer1(g + 1, q + b, 1 - b)
                if before_it:
                    aggregate(g - 1, 1 - b)

            layer1(0, 0, 0)
            pe_group(0, 0, 0, before_it=False)
            single(pe_group, 1, 2)
            pairs(pe, pe_group, 3, GB - 1)
            single(pe_group, GB)
            pe.wait_ge(msg_done, 2 * GB)
            pe.wait_ge(added, GT * GB)
            part_rows(1)
            single(pe_group, GB + 1)
            pairs(pe, pe_group, GB + 2, G0 - 3)
            single(pe_group, G0 - 2)
            pe_group(G0 - 1, G0 // 2, 0, after_it=False)
            layer5(G0 - 1)
            aggregate(G0 - 1, 0)

            with pe.Fori(0, CHUNKS) as c:
                pe.wait_ge(nv, NV * c + NV_OUT)
                for j in range(2 * CB):
                    last = nc.tensor.transpose(ps[:, j // 4, (j % 4) * P:(j % 4 + 1) * P],
                                               chunk[2][:, j * P:(j + 1) * P], ident[:, :])
                    if j % 4 == 3 or j == 2 * CB - 1:
                        last.then_inc(npe, 1)
                for j in range(CB):
                    if j % 2 == 0:
                        pe.wait_ge(nact, NACT * c + NACT_STD + j // 2 + 1)
                    o = ps[:, 4 + j // 2, (j % 2) * H:(j % 2 + 1) * H]
                    for k in range(2):
                        mm(o, chunk[3][:, (2 * j + k) * P:(2 * j + k + 1) * P], gws[:, k, :],
                           start=(k == 0), stop=False)
                    last = mm(o, ones3[:, :], bias3[:, 2, :], start=False, stop=True)
                    if j % 2 or j == CB - 1:
                        last.then_inc(npe, 1)

            for k in range(2):
                def aggregate2(g, q, b):
                    pe.wait_ge(hot2_done[k], g + 1)
                    pe.wait_ge(scaled[k], g + 1)
                    if not (isinstance(g, int) and g < 2):
                        pe.wait_ge(added2[k], GT * (g - 1))
                    for t in range(GT):
                        last = mm(ps[:, 2 * b + t // 2, (t % 2) * H:(t % 2) * H + ACW], hot[b][:, t, :],
                                  msg2[b][:, t, :], start=True, stop=True)
                        if t % 2:
                            last.then_inc(agg2_mm[k], 1)
                if k:
                    pe.wait_ge(added2[0], GT * G0)
                all_groups(pe, aggregate2, GROUPS[k])

        @block.vector
        def _(dve):
            V = nc.vector

            def stepper(s, start=0):
                n = [0]

                def step(ins):
                    n[0] += 1
                    ins.then_inc(s, 1)
                    dve.wait_ge(s, start + n[0])
                step.count = n
                return step


            for f, v in enumerate((-1.0, float(PAD_NODE), 0.0, 0.0)):
                V.memset(rec[0][:, 0:max(ST), f], v).then_inc(default_set, 1)
            V.memset(w1d[:, :], 0.0).then_inc(default_set, 1)
            V.memset(offs[:, NB:NB2], 0.0)

            step = stepper(chain)
            dve.wait_ge(edges_in, 48)
            step(V.tensor_scalar(run, wt, 0.5 / CUTOFF, None, ALU.mult))
            step(V.scalar_tensor_tensor(eq, run, -1.0, run, ALU.mult, ALU.max))
            step(V.tensor_scalar(run, eq, ROUND, None, ALU.add))
            step(V.tensor_scalar(run, run, -ROUND, None, ALU.add))
            step(V.tensor_tensor(eq, eq, run, ALU.subtract))
            step(V.scalar_tensor_tensor(run, eq, -1.0, eq, ALU.mult, ALU.max))
            V.tensor_scalar(eq, run, -2.0 * math.pi, 0.5 * math.pi, ALU.mult, ALU.add).then_inc(envelope, 1)
            step(V.tensor_scalar(blk, wt, CUTOFF, None, ALU.is_lt))
            srec = [t.rearrange("p (e f) -> p e f", f=4) for t in stage_rec]
            dve.wait_ge(envelope, 2)
            step(V.scalar_tensor_tensor(srec[0][:, :, 3], run, 1.0, blk, ALU.add, ALU.mult))
            V.memset(srec[1][:, :, 3], 0.0)

            def prepare(k):
                step(V.tensor_scalar(eq.bitcast(i32), key_i[k], 7, None, ALU.logical_shift_right))
                step(V.tensor_copy(blk, eq.bitcast(i32)))
                step(V.tensor_scalar(run.bitcast(i32), key_i[k], P - 1, None, ALU.bitwise_and))
                V.tensor_copy(srec[k][:, :, 0], run.bitcast(i32))
                V.tensor_copy(srec[k][:, :, 1], key_i[1 - k])
                step(V.tensor_copy(srec[k][:, :, 2], wt))

            def columns(s, t):
                return t[:, COL0[s]:COL0[s] + COLS[s]]

            def count(s):
                done = step.count[0]
                with dve.Fori(0, NB2 // 2) as i:
                    for j, scratch in enumerate((eq, run)):
                        dve.wait_ge(chain, done + 2 * i + (j - 1))
                        V.tensor_scalar(columns(s, scratch), columns(s, blk), lane[:, bass.ds(2 * i + j, 1)],
                                        None, ALU.is_equal, ALU.add,
                                        accum_out=cnt[:, bass.ds(2 * i + j, 1)]).then_inc(chain, 1)
                step.count[0] += NB2
                dve.wait_ge(chain, step.count[0])
                V.memset(columns(s, rank), 0.0).then_inc(counted, 1)
                dve.wait_ge(prefix_mm, s + 1)
                step(V.tensor_scalar(nt_i[:, :], ps[:, 6, 64:64 + NB], float(P - 1), None, ALU.add))
                step(V.tensor_scalar(nt_i[:, :], nt_i[:, :], 7, None, ALU.logical_shift_right))
                step(V.tensor_copy(tot[:, :], nt_i[:, :]))
                step(V.tensor_tensor_scan(start[:, :], tot[:, :], tot[:, :], 0.0, ALU.add, ALU.max))
                step(V.tensor_tensor(start[:, :], start[:, :], tot[:, :], ALU.subtract))
                step(V.scalar_tensor_tensor(offs[:, 0:NB], start[:, :], float(P), ps[:, 6, 0:NB], ALU.mult, ALU.add))
                step(V.tensor_scalar(ntc_i[:, :], ps[0:NB, 6, 128:129], float(P - 1), None, ALU.add))
                step(V.tensor_scalar(ntc_i[:, :], ntc_i[:, :], 7, None, ALU.logical_shift_right))
                V.tensor_copy(ntc[:, :], ntc_i[:, :]).then_inc(tiles_set, 1)
                dve.wait_ge(starts_mm, s + 1)
                step(V.tensor_copy(startc[:, :], ps[0:NB, 6, 130:131]))
                V.tensor_scalar(reached[:, 0:ST[s]], tile_no[0:NB, 0:ST[s]], startc[:, 0:1], None,
                                ALU.is_ge).then_inc(reached_set, 1)
                dve.wait_ge(table_mm, s + 1)
                for row, width in (((0, H), (1, ACW)) if s < 2 else ((2, ACW),)):
                    p = TROW[row]
                    for bank, lo, hi in table_parts(s):
                        last = V.tensor_scalar(table[p:p + 1, TILE0[s] + lo:TILE0[s] + hi],
                                               ps[p:p + 1, bank, 0:hi - lo], -1.0, float(width),
                                               ALU.add, ALU.mult)
                last.then_inc(table_set, 1)
                dve.wait_ge(table_set, s + 1)

            def ranks(s):
                n = COLS[s]
                sets = [(columns(s, eq), columns(s, run), columns(s, rank)), (eq1[:, 0:n], run1[:, 0:n], rank1[:, 0:n])]
                step(V.memset(sets[1][2], 0.0))
                done = step.count[0]
                with dve.Fori(0, NB2 // 2) as i:
                    def after(n):
                        dve.wait_ge(chain, done + 8 * i + n)

                    for j, (e, r, _) in enumerate(sets):
                        after(j - 3)
                        V.tensor_scalar(e, columns(s, blk), lane[:, bass.ds(2 * i + j, 1)], None,
                                        ALU.is_equal).then_inc(chain, 1)
                    for j, (e, r, _) in enumerate(sets):
                        after(j + 1)
                        V.tensor_tensor_scan(r, e, e, offs[:, bass.ds(2 * i + j, 1)],
                                             ALU.add, ALU.max).then_inc(chain, 1)
                    for j, (e, r, _) in enumerate(sets):
                        after(j + 3)
                        V.tensor_tensor(r, r, e, ALU.mult).then_inc(chain, 1)
                    for j, (e, r, a) in enumerate(sets):
                        after(j + 5)
                        V.tensor_tensor(a, a, r, ALU.add).then_inc(chain, 1)
                step.count[0] += 4 * NB2
                dve.wait_ge(chain, step.count[0])

            def addresses(step, s, second_rank):
                slot_i, lane_i, tile_i = (columns(s, t).bitcast(i32) for t in (eq, run, blk))
                if second_rank is None:
                    step(V.tensor_scalar(slot_i, columns(s, rank), -1.0, None, ALU.add))
                else:
                    step(V.scalar_tensor_tensor(slot_i, columns(s, rank), -1.0, second_rank, ALU.add, ALU.add))
                step(V.tensor_scalar(lane_i, slot_i, P - 1, None, ALU.bitwise_and))
                step(V.tensor_scalar(tile_i, slot_i, 7, None, ALU.logical_shift_right))
                V.scalar_tensor_tensor(columns(s, stage_adr[s // 2]), lane_i, float(ST[s]), tile_i,
                                       ALU.mult, ALU.add).then_inc(sorted_key, 1)
                dve.wait_ge(sorted_key, s + 1)

            dve.wait_ge(consts, 6)
            dve.wait_ge(weights_in, 16 * n_weights)
            V.tensor_scalar(negc[:, :], col[:, 0:1], -1.0, None, ALU.mult)
            step(V.scalar_tensor_tensor(zscale[:, :], col[:, 1:2], -1.0, col[:, 1:2], ALU.mult, ALU.max))
            step(V.tensor_scalar(zscale[:, :], zscale[:, :], EPS_W, None, ALU.add))
            step(V.reciprocal(zscale[:, :], zscale[:, :]))
            step(V.tensor_tensor(zscale[:, :], zscale[:, :], zscale[:, :], ALU.mult))
            V.tensor_scalar(zscale[:, :], zscale[:, :], 0.25, None, ALU.mult).then_inc(params_set, 1)
            dve.wait_ge(fused_mm, 1)
            V.tensor_copy(w23[:, :], ps[:, 4, 0:H])
            V.tensor_tensor(b23[:, :], ps[:, 5, 0:2], col[:, 3:5], ALU.add).then_inc(params_set, 1)
            step(V.tensor_copy(part[0][:, :], r3[:, :]))
            step(V.tensor_tensor(r3b[0][:, :], r3[:, :], part[0][:, :], ALU.subtract))
            step(V.tensor_copy(part[1][:, :], r3b[0][:, :]))
            step(V.tensor_tensor(r3b[1][:, :], r3b[0][:, :], part[1][:, :], ALU.subtract))
            step(V.tensor_copy(part[2][:, :], r3b[1][:, :]))
            step(V.tensor_scalar(r3b[0][:, :], part[0][:, :], ident[0:3, 0:1], None, ALU.mult))
            for k in (1, 2):
                o = r3b[1][:, :] if k == 1 else bias3[:, :, :].rearrange("p a b -> p (a b)")
                i = r3b[0][:, :] if k == 1 else r3b[1][:, :]
                last = V.scalar_tensor_tensor(o, part[k][:, :], ident[0:3, k:k + 1], i, ALU.mult, ALU.add)
                if k == 1:
                    step(last)
            last.then_inc(biases_set, 1)

            prepare(0)
            for s in range(2):
                count(s)
                ranks(s)
                addresses(step, s, rank1[:, 0:COLS[s]])
            prepare(1)
            count(2)
            dve.sem_inc(rank_chain)
            dve.wait_ge(rec_in[0], 16)
            dve.wait_ge(consts, 7)

            def radial_basis(g, q, b):
                dve.wait_ge(tanh_done, g + 1)
                V.tensor_scalar(up1, th[b], 1.0, None, ALU.add).then_inc(rbf_chain, 1)
                dve.wait_ge(rbf_chain, 2 * g + 1)
                if not (isinstance(g, int) and g == 0):
                    dve.wait_ge(rbf_done, g)
                V.reciprocal(rcp, up1).then_inc(rbf_chain, 1)
                dve.wait_ge(rbf_chain, 2 * g + 2)
                if not (isinstance(g, int) and g < 2):
                    dve.wait_ge(l1_mm, g - 1)
                V.scalar_tensor_tensor(rbf[b], rcp, -0.5, de[b][:, 1, :], ALU.add, ALU.mult).then_inc(rbf_done, 1)

            def one_hot(k, g, b, s):
                V.tensor_tensor(hot[b][:, :, :], lane[:, None, :].to_broadcast([P, GT, P]),
                                rec[k][:, bass.ds(g * GT, GT), 0:1].to_broadcast([P, GT, P]),
                                ALU.is_equal).then_inc(s, 1)

            def messages(g, q, b):
                dve.wait_ge(gathered[b], 16 * GT * q + 16 * GT)
                for h in range(2):
                    dve.wait_ge(l5_mm, 2 * g + h + 1)
                    V.tensor_tensor(msg[:, 2 * h:2 * h + 2, :].rearrange("p a b -> p (a b)"), ps[:, 5 + h, :],
                                    gath[b][:, 2 * h:2 * h + 2, :].rearrange("p a b -> p (a b)"),
                                    ALU.mult).then_inc(msg_done, 1)

            def places_of(row, width, g):
                return nc.values_load_multi_w_load_instructions(
                    table[TROW[row]:TROW[row] + 1, bass.ds(g * GT, GT)], [mybir.EngineType.DVE],
                    min_val=0, max_val=(NB - 1) * width,
                    skip_runtime_bounds_check_because="a count of at most NB block starts, less one, and the "
                                                      "first block starts at tile 0")[1]

            def add_up(g):
                places = places_of(0, H, g)
                for t in range(GT):
                    if not (isinstance(g, int) and g == 0 and t == 0):
                        dve.wait_ge(added, GT * g + t)
                    dve.wait_ge(agg_mm, 2 * g + t // 2 + 1)
                    rows_of = agg[:, bass.ds(places[t], H)]
                    V.tensor_tensor(rows_of, rows_of, ps[:, 7 * (1 - t // 2), (t % 2) * H:(t % 2 + 1) * H],
                                    ALU.add).then_inc(added, 1)

            def rank_turn(g, n):
                at = g - GR
                dve.wait_ge(rank_chain, 4 * at + n + 1)
                ins = (V.tensor_scalar(eq, blk, lane[:, bass.ds(at, 1)], None, ALU.is_equal) if n == 0 else
                       V.tensor_tensor_scan(run, eq, eq, offs[:, bass.ds(at, 1)], ALU.add, ALU.max) if n == 1 else
                       V.tensor_tensor(run, run, eq, ALU.mult) if n == 2 else
                       V.tensor_tensor(rank, rank, run, ALU.add))
                ins.then_inc(rank_chain, 1)

            def dve_group(ahead=True, before_it=True, ranking=False):
                def body(g, q, b):
                    if ranking:
                        rank_turn(g, 0)
                    if ahead:
                        radial_basis(g + 2, q + 1, b)
                    if ranking:
                        rank_turn(g, 1)
                    one_hot(0, g, b, hot_done)
                    if before_it:
                        messages(g - 1, q + b - 1, 1 - b)
                        if ranking:
                            rank_turn(g, 2)
                        add_up(g - 1)
                    if ranking:
                        rank_turn(g, 3)
                return body

            radial_basis(0, 0, 0)
            radial_basis(1, 0, 1)
            single(dve_group(before_it=False), 0)
            single(dve_group(), 1, 2)
            pairs(dve, dve_group(ranking=True), GR, GR + NB - 2)
            single(dve_group(ranking=True), GR + NB - 1)
            dve.wait_ge(rank_chain, 4 * NB + 1)
            addresses(stepper(rank_chain, 4 * NB + 1), 2, None)
            single(dve_group(), GR + NB)
            pairs(dve, dve_group(), GR + NB + 1, G0 - 3)
            single(dve_group(ahead=False), G0 - 2, G0 - 1)
            messages(G0 - 1, G0 // 2, 0)
            add_up(G0 - 1)

            for k in range(2):
                V.memset(msg2[k][:, :, HALF:ACW], 1.0)
            for b in range(2):
                dve.wait_ge(scattered[2][b], 16 * SU * slot_uses(UNITS[2], b))

            def by_block(t):
                return t.rearrange("p (j n) -> p j n", j=CB)

            def moments(step, src):
                for j in range(CB):
                    last = V.bn_stats(stats[:, j, :], by_block(src)[:, j, :])
                step(last)
                dve.sem_inc(carrier)
                for j in range(CB):
                    last = V.bn_aggr(mv[:, j, :], stats[:, j, :])
                step(last)
                step(V.tensor_scalar(var_eps[:, :], mv[:, :, 1], EPS_LN, None, ALU.add))

            def normalise(step, dst, src):
                step(V.reciprocal(rstd[:, :], std[:, :]))
                for j in range(CB):
                    last = V.tensor_scalar(by_block(dst)[:, j, :], by_block(src)[:, j, :], mv[:, j, 0:1],
                                           rstd[:, j:j + 1], ALU.subtract, ALU.mult)
                step(last)

            def node_chunk(c):
                step = stepper(nv, NV * c)
                dve.wait_ge(x_in, 16 * c + 16)
                step(V.tensor_tensor(chunk[1], chunk[0], agg[:, bass.ds(c * (CB * H), CB * H)], ALU.add))
                moments(step, chunk[1])
                assert step.count[0] == NV_VAR1
                dve.wait_ge(nact, NACT * c + NACT_STD)
                normalise(step, chunk[2], chunk[1])
                step(V.tensor_tensor(by_block(chunk[2]), by_block(chunk[2]), gb[:, 0:1, :].to_broadcast([P, CB, H]), ALU.mult))
                step(V.tensor_tensor(by_block(chunk[2]), by_block(chunk[2]), gb[:, 1:2, :].to_broadcast([P, CB, H]), ALU.add))
                assert step.count[0] == NV_OUT
                dve.wait_ge(nact, NACT * c + NACT_GATE)
                step(V.scalar_tensor_tensor(chunk[6], chunk[4], 1.0, chunk[2], ALU.add, ALU.mult))
                step(V.scalar_tensor_tensor(chunk[1], chunk[6], 0.5, chunk[0], ALU.mult, ALU.add))
                moments(step, chunk[1])
                assert step.count[0] == NV_VAR2
                dve.wait_ge(nact, NACT * c + NACT_STD2)
                if not isinstance(c, int):
                    dve.wait_ge(x1_out, 32 * c)
                    dve.wait_ge(nact, NACT * c)
                normalise(step, chunk[5], chunk[1])
                assert step.count[0] == NV

            chunks(dve, node_chunk)
            dve.wait_ge(x1_out, 32 * CHUNKS)
            dve.wait_ge(nact, NACT * CHUNKS)
            V.memset(arena1[:, 0:2 * NB * ACW], 0.0)
            dve.wait_ge(rec_in[2], 16)

            for k in range(2):
                def scale(g, q, b):
                    dve.wait_ge(gathered2[k][b], 16 * GT * q + 16 * GT)
                    V.tensor_tensor(msg2[b][:, :, 0:HALF], gath[b][:, :, 0:HALF],
                                    rec[k][:, bass.ds(g * GT, GT), 2:3].to_broadcast([P, GT, HALF]),
                                    ALU.mult).then_inc(scaled[k], 1)

                def sums(g, b):
                    places = places_of(1 + k, ACW, g)
                    for t in range(GT):
                        if not (isinstance(g, int) and g == 0 and t == 0):
                            dve.wait_ge(added2[k], GT * g + t)
                        dve.wait_ge(agg2_mm[k], 2 * g + t // 2 + 1)
                        rows_of = acc[k][:, bass.ds(places[t], ACW)]
                        V.tensor_tensor(rows_of, rows_of,
                                        ps[:, 2 * b + t // 2, (t % 2) * H:(t % 2) * H + ACW],
                                        ALU.add).then_inc(added2[k], 1)

                def group2(g, q, b):
                    one_hot(k, g, b, hot2_done[k])
                    scale(g, q, b)
                    if not (isinstance(g, int) and g == 0):
                        sums(g - 1, 1 - b)

                all_groups(dve, group2, GROUPS[k])
                sums(GROUPS[k] - 1, 0)

            step = stepper(chain, step.count[0])
            step.count[0] = 0
            for k in range(2):
                deg = acc[k].rearrange("p (n f) -> p n f", f=ACW)[:, :, HALF]
                step(V.tensor_scalar(rdeg[k][:, :], deg, 1.0, None, ALU.max))
                step(V.reciprocal(rdeg[k][:, :], rdeg[k][:, :]))

            def last_chunk(c):
                step = stepper(fv, FV * c)
                for k in range(2):
                    sums_of = acc[k][:, bass.ds(c * (CB * ACW), CB * ACW)].rearrange("p (j f) -> p j f", f=ACW)
                    last = V.tensor_tensor(by_block(last_c[1])[:, :, k * HALF:(k + 1) * HALF], sums_of[:, :, 0:HALF],
                                           rdeg[k][:, bass.ds(c * CB, CB), None].to_broadcast([P, CB, HALF]),
                                           ALU.mult)
                step(last)
                step(V.tensor_tensor(last_c[0], last_c[1], agg[:, bass.ds(c * (CB * H), CB * H)], ALU.add))
                moments(step, last_c[0])
                assert step.count[0] == FV_VAR
                dve.wait_ge(fact, c + 1)
                if not isinstance(c, int):
                    dve.wait_ge(out_done, 16 * c)
                normalise(step, last_c[2], last_c[0])
                assert step.count[0] == FV

            chunks(dve, last_chunk)


def kernel(x, src, dst, edge_weight, L0_gnn_centers, L0_gnn_widths, L0_gnn_rbf_w1, L0_gnn_rbf_b1,
           L0_gnn_rbf_w2, L0_gnn_rbf_b2, L0_gnn_filt_w1, L0_gnn_filt_b1, L0_gnn_filt_w2, L0_gnn_filt_b2,
           L0_gnn_filt_w3, L0_gnn_filt_b3, L0_gnn_node_w, L0_gnn_node_b, L0_gnn_ln_g, L0_gnn_ln_b,
           L0_gnn_gate_w, L0_gnn_gate_b):
    import numpy as np
    import concourse.bacc as bacc
    from concourse.bass_utils import run_bass_kernel_spmd

    def arr(a):
        return np.ascontiguousarray(np.asarray(a))

    def edges(a, pad):
        a = np.asarray(a)
        return np.concatenate([a, np.full(P * EC - E, pad, a.dtype)]).reshape(P, EC)

    xp = np.concatenate([np.asarray(x), np.zeros((NP - N, H), np.float32)])
    twice = lambda a: np.tile(np.asarray(a), 2)
    f_b1, f_b2 = np.asarray(L0_gnn_filt_b1), np.asarray(L0_gnn_filt_b2)
    cols = np.stack([twice(L0_gnn_centers), twice(L0_gnn_widths), twice(L0_gnn_rbf_b1), f_b1[:P], f_b1[P:],
                     f_b2[:P], f_b2[P:], twice(L0_gnn_rbf_b2)], axis=1)
    rows = np.tile(np.concatenate([np.asarray(a) for a in (L0_gnn_filt_b3, L0_gnn_node_b, L0_gnn_gate_b)]), (3, 1))
    arrays = {
        "x": xp, "xT": arr(xp.T),
        "src": edges(src, PAD_NODE), "dst": edges(dst, PAD_NODE), "wgt": edges(edge_weight, 0.0),
        "cols": arr(cols), "rows": arr(rows), "ln_gb": np.stack([np.asarray(L0_gnn_ln_g), np.asarray(L0_gnn_ln_b)]),
        "w1": arr(L0_gnn_rbf_w1), "w2T": arr(np.tile(np.asarray(L0_gnn_rbf_w2).T, (1, 2))),
        "f1": arr(L0_gnn_filt_w1), "f2": arr(L0_gnn_filt_w2), "f3": arr(L0_gnn_filt_w3),
        "node_w": arr(L0_gnn_node_w), "gate_w": arr(L0_gnn_gate_w),
    }
    nc = bacc.Bacc("TRN2", target_bir_lowering=False, num_devices=1)
    args = [nc.dram_tensor(k, a.shape, mybir.dt.from_np(a.dtype), kind="ExternalInput").ap()
            for k, a in arrays.items()]
    out = nc.dram_tensor("out", (NP, H), mybir.dt.float32, kind="ExternalOutput").ap()
    build(nc, *args, out)
    result = run_bass_kernel_spmd(nc, [arrays], core_ids=[0])
    return result.results[0]["out"][:N]
```

```python
import math
from contextlib import ExitStack

import concourse.bass as bass
import concourse.mybir as mybir

P = 128
N = 6250
H = 256
HALF = H // 2
R = 64
NB = -(-N // P)
NP = NB * P
E = 100000
GT = 4
SU = 6
EC = -(-E // (P * SU)) * SU
CA = EC * 11 // 30 // (2 * SU) * 2 * SU
COLS = (CA, EC - CA, EC)
COL0 = (0, CA, 0)
UNITS = tuple(n // SU for n in COLS)
ST = tuple(-(-((P * n + NB * (P - 1)) // P) // GT) * GT for n in COLS)
TILE0 = (0, ST[0], 0)
TILES = (ST[0] + ST[1], ST[2])
GROUPS = tuple(t // GT for t in TILES)
G0, G1 = GROUPS
GA = ST[0] // GT
GB = UNITS[1] - 2
GR = 3
BR = NB - (GA - GR) // 2
NB2 = NB + NB % 2
assert UNITS[0] % 4 == 0 and GA % 2 == 0 and GB % 2 == 1 and GB + 1 < GA and GA + UNITS[2] < G0
assert G0 % 2 == 1 and G1 % 2 == 1 and BR > 0 and NB % 2 == 1
PAD_NODE = NP - 1
CB = 7
CHUNKS = NB // CB
ACW = HALF + 1
GW = GT * P // 2
CUTOFF = 10.0
EPS_W = 1e-5
EPS_LN = 1e-5
VB = 4
ROUND = 1.5 * 2.0 ** 23


def build(nc, x, xT, src, dst, wgt, cols, rows, ln_gb, w1, w2T, f1, f2, f3, node_w, gate_w, out):
    f32, bf16, i32 = mybir.dt.float32, mybir.dt.bfloat16, mybir.dt.int32
    ALU, ACT = mybir.AluOpType, mybir.ActivationFunctionType

    y_rows = nc.dram_tensor("y_rows", (NP, H), f32).ap()
    x1_half = [nc.dram_tensor(f"x1_half{k}", (NP, HALF), f32).ap() for k in range(2)]
    records = [nc.dram_tensor(f"records{s}", (P * ST[s], 4), f32).ap() for s in range(3)]
    slot_rows = nc.dram_tensor("slot_rows", (2, TILES[0] * P), f32).ap()

    with ExitStack() as ctx:
        def sb(name, shape, dt=f32):
            return ctx.enter_context(nc.sbuf_tensor(name, shape, dt))

        def sem(name):
            return ctx.enter_context(nc.semaphore(name))

        lane = sb("lane", [P, P])
        ident = sb("ident", [P, P])
        before = sb("before", [P, P])
        ones = sb("ones", [P, P])
        ones3 = sb("ones3", [3, P], bf16)
        w1d = sb("w1d", [P, P])
        w2t = sb("w2t", [R, P])
        f1s = sb("f1s", [R, H])
        w23 = sb("w23", [P, H])
        f2s = sb("f2s", [P, 2, H])
        f3s = sb("f3s", [P, 2, H])
        nws = sb("nws", [P, 2, H])
        gws = sb("gws", [P, 2, H])
        gb = sb("gb", [P, 2, H])
        b3 = sb("b3", [P, H])
        col = sb("col", [P, 8])
        negc = sb("negc", [P, 1])
        zscale = sb("zscale", [P, 1])
        b23 = sb("b23", [P, 2])
        r3 = sb("r3", [3, 3 * H])
        r3b = [sb(f"r3b{k}", [3, 3 * H]) for k in range(2)]
        part = [sb(f"part{k}", [3, 3 * H], bf16) for k in range(3)]
        bias3 = sb("bias3", [3, 3, H], bf16)

        agg = sb("agg", [P, NB * H])
        rec = [sb(f"rec{k}", [P, TILES[k], 4]) for k in range(2)]
        table = sb("table", [P, TILES[0]], i32)
        TROW = (0, 32, 64)
        cnt = sb("cnt", [P, NB2])
        tot = sb("tot", [P, NB])
        start = sb("start", [P, NB])
        nt_i = sb("nt_i", [P, NB], i32)
        offs = sb("offs", [P, NB2])
        ntc = sb("ntc", [NB, 1])
        ntc_i = sb("ntc_i", [NB, 1], i32)
        startc = sb("startc", [NB, 1])

        A1 = 17 * EC
        arena1 = sb("arena1", [P, A1])
        at = 0

        def take(n):
            nonlocal at
            at += n
            return arena1[:, at - n:at]

        stage_rec = [take(4 * EC) for _ in range(2)]
        stage_adr = [take(EC).bitcast(i32) for _ in range(2)]
        key_i = [take(EC).bitcast(i32) for _ in range(2)]
        wt = take(EC)
        blk, eq, run, rank = take(EC), take(EC), take(EC), take(EC)
        acc = [arena1[:, k * NB * ACW:(k + 1) * NB * ACW] for k in range(2)]


        arena2 = sb("arena2", [P, 33 * GW])
        at2 = 0

        def ring(*shape):
            nonlocal at2
            n = math.prod(shape)
            v = arena2[:, at2:at2 + n]
            at2 += n
            if len(shape) == 2:
                v = v.rearrange("p (a b) -> p a b", a=shape[0])
            if len(shape) == 3:
                v = v.rearrange("p (a b c) -> p a b c", a=shape[0], b=shape[1])
            return v

        gath = [ring(GT, H) for _ in range(2)]
        de = [ring(2, GW) for _ in range(2)]
        sq = ring(GW)
        th = [ring(GW) for _ in range(2)]
        up1 = ring(GW)
        rcp = ring(GW)
        rbf = [ring(GW) for _ in range(2)]
        s1 = [ring(GW) for _ in range(2)]
        s2 = ring(2, GT * P)
        s3 = ring(2, GT * P)
        msg = ring(GT, H)
        assert at2 == 33 * GW and A1 >= 7 * CB * H
        chunk = ([arena1[:, k * CB * H:(k + 1) * CB * H] for k in range(7)] +
                 [arena2[:, k * CB * H:(k + 1) * CB * H] for k in range(4)])
        x_c, h_c, x1_c = chunk[0:3], chunk[3:6], chunk[6:8]
        tr_c, gate_c, res_c = chunk[8:11]
        last_c = [arena2[:, k * CB * H:(k + 1) * CB * H] for k in range(3)]
        xt_c = [t.rearrange("p (k n) -> p k n", k=2) for t in (last_c[0], agg[:, 0:CB * H])]
        y_c = [t.rearrange("p (j n) -> p j n", j=CB) for t in (last_c[1], agg[:, CB * H:2 * CB * H])]
        tile_no = arena2[:, 2 * CB * H:2 * CB * H + TILES[0]]
        reached = arena2[0:NB, 2 * CB * H + TILES[0]:2 * CB * H + 2 * TILES[0]]
        at2 = 2 * CB * H + 2 * TILES[0]
        eq1, run1, rank1 = ring(COLS[1]), ring(COLS[1]), ring(COLS[1])
        assert at2 <= 33 * GW
        RB = -(-max(ST[0], ST[1]) // P)
        rows_of_slots = sb("rows_of_slots", [P, 2, RB, P])
        msg2 = [(s2, s3)[k].rearrange("p a b -> p (a b)")[:, 0:GT * ACW].rearrange("p (t f) -> p t f", t=GT)
                for k in range(2)]
        hot = [sb(f"hot{k}", [P, GT, P]) for k in range(2)]
        idx = [sb(f"idx{k}", [P, GT], i32) for k in range(2)]
        sc_rec = [sb(f"sc_rec{k}", [P, SU, 4]) for k in range(2)]
        sc_adr = [sb(f"sc_adr{k}", [P, SU], i32) for k in range(2)]
        stats = sb("stats", [P, CB, 6])
        mv = sb("mv", [P, CB, 2])
        mv1 = [sb(f"mv1{b}", [P, CB, 2]) for b in range(3)]
        rstd1 = [sb(f"rstd1{b}", [P, CB]) for b in range(3)]
        shift1 = [sb(f"shift1{b}", [P, CB]) for b in range(3)]
        var_eps1 = sb("var_eps1", [P, CB])
        std1 = sb("std1", [P, CB])
        var_eps = sb("var_eps", [P, CB])
        std = sb("std", [P, CB])
        rstd = sb("rstd", [P, CB])
        flat = rows_of_slots[:, :, :, :].rearrange("p a b c -> p (a b c)")
        assert 2 * RB * P >= 18 * NB
        half_stats = flat[:, 0:12 * NB].rearrange("p (n k f) -> p n k f", k=2, f=6)
        last_mv = flat[:, 12 * NB:14 * NB].rearrange("p (n f) -> p n f", f=2)
        last_eps, last_sd, last_inv, last_shift = (flat[:, i * NB:(i + 1) * NB] for i in range(14, 18))
        rdeg = [sb(f"rdeg{k}", [P, NB]) for k in range(2)]

        ps = ctx.enter_context(nc.psum_tensor("ps", [P, 8, 512], f32))

        edges_in, weights_in = sem("edges_in"), sem("weights_in")
        default_set, default_out = sem("default_set"), sem("default_out")
        consts = sem("consts")
        carrier = sem("carrier")
        fused_mm, params_set, biases_set = sem("fused_mm"), sem("params_set"), sem("biases_set")
        counted, prefix_mm, tiles_set = sem("counted"), sem("prefix_mm"), sem("tiles_set")
        starts_mm, reached_set, table_mm, table_set = (
            sem("starts_mm"), sem("reached_set"), sem("table_mm"), sem("table_set"))
        envelope = sem("envelope")
        chain = sem("chain")
        sorted_key = sem("sorted_key")
        y_mm, y_evac = sem("y_mm"), sem("y_evac")
        xt_in = [sem(f"xt_in{b}") for b in range(2)]
        y_out = [sem(f"y_out{b}") for b in range(2)]
        sc_staged = sem("sc_staged")
        scattered = [[sem(f"scattered{k}{b}") for b in range(2)] for k in range(3)]
        rec_in = [sem(f"rec_in{s}") for s in range(3)]
        rank_chain = sem("rank_chain")
        rows_mm, rows_evac, rows_out = sem("rows_mm"), sem("rows_evac"), sem("rows_out")
        de_in = [sem(f"de_in{b}") for b in range(2)]
        squared, tanh_done, rbf_done = sem("squared"), sem("tanh_done"), sem("rbf_done")
        rbf_chain = sem("rbf_chain")
        l1_mm, l23_mm, l4_mm, l5_mm = sem("l1_mm"), sem("l23_mm"), sem("l4_mm"), sem("l5_mm")
        s1_done, s2_done, s3_done = sem("s1_done"), sem("s2_done"), sem("s3_done")
        idx_staged = sem("idx_staged")
        gathered = [sem(f"gathered{b}") for b in range(2)]
        biased = sem("biased")
        hot_done, msg_done, agg_mm, added = sem("hot_done"), sem("msg_done"), sem("agg_mm"), sem("added")
        x1_set = sem("x1_set")
        x_in = [sem(f"x_in{b}") for b in range(3)]
        x1_out = [sem(f"x1_out{b}") for b in range(2)]
        nv = sem("nv")
        var1_set, std1_set, rstd1_set, affine, gained, normed = (
            sem("var1_set"), sem("std1_set"), sem("rstd1_set"), sem("affine"), sem("gained"), sem("normed"))
        tr_mm, tr_evac, gate_mm, gate_evac, gated = (
            sem("tr_mm"), sem("tr_evac"), sem("gate_mm"), sem("gate_evac"), sem("gated"))
        var2_set, std2_set = sem("var2_set"), sem("std2_set")
        idx2_staged = [sem(f"idx2_staged{k}") for k in range(2)]
        gathered2 = [[sem(f"gathered2{k}{b}") for b in range(2)] for k in range(2)]
        hot2_done = [sem(f"hot2_done{k}") for k in range(2)]
        scaled = [sem(f"scaled{k}") for k in range(2)]
        agg2_mm = [sem(f"agg2_mm{k}") for k in range(2)]
        added2 = [sem(f"added2{k}") for k in range(2)]
        mean_steps = sem("mean_steps")
        merged = sem("merged")
        last_var, last_std, last_rstd = sem("last_var"), sem("last_std"), sem("last_rstd")
        last_vector, last_scalar, out_done = sem("last_vector"), sem("last_scalar"), sem("out_done")

        block = ctx.enter_context(nc.Block())

        y_v = y_rows.rearrange("(c j p) n -> c p j n", p=P, j=CB)
        x_v = x.rearrange("(c j p) n -> c p j n", p=P, j=CB)
        out_v = out.rearrange("(c j p) n -> c p j n", p=P, j=CB)
        x1_v = [t.rearrange("(c j p) n -> c p j n", p=P, j=CB) for t in x1_half]
        xT_v = xT.rearrange("(k p) (c n) -> c p k n", p=P, c=CHUNKS)
        rec_v = [t.rearrange("(p t) f -> p t f", p=P) for t in records]

        def hold(eng, s, value):
            eng.wait_ge(s, value)
            eng.sem_inc(carrier)

        def pairs(eng, body, lo, hi):
            with eng.Fori((lo + 1) // 2, hi // 2 + 1) as i:
                body(2 * i - 1, i - 1, 1)
                body(2 * i, i, 0)

        def by_block(t):
            return t.rearrange("p (j n) -> p j n", j=CB)

        def single(body, *groups):
            for g in groups:
                body(g, g // 2, g % 2)

        def all_groups(eng, body, n):
            single(body, 0, 1, 2)
            pairs(eng, body, 3, n - 3)
            single(body, n - 2, n - 1)

        def slot_uses(n, b):
            return (n + 1 - b) // 2

        def table_parts(s):
            n = -(-ST[s] // 512)
            cuts = [ST[s] * i // n for i in range(n + 1)]
            return [(5 + 2 * i, cuts[i], cuts[i + 1]) for i in range(n)]

        def row_blocks(s):
            for f in range(2):
                for j in range(-(-ST[s] // P)):
                    bank, c = (5 + f, j * P) if j < 4 else (7, f * P)
                    yield f, j, min(P, ST[s] - j * P), bank, c

        n_weights = 13

        @block.sync
        def _(sp):
            for t, d in ((key_i[0], src), (key_i[1], dst), (wt, wgt)):
                sp.dma_start(t, d).then_inc(edges_in, 16)
            for t, d in ((w2t, w2T), (f1s, f1), (col, cols), (r3, rows)):
                sp.dma_start(t[:, :], d).then_inc(weights_in, 16)
            for t, d in ((f2s, f2), (f3s, f3), (nws, node_w), (gws, gate_w)):
                sp.dma_start(t[:, :, :], d.rearrange("(k p) n -> p k n", p=P)).then_inc(weights_in, 16)
            for k in range(2):
                sp.dma_start(gb[:, k, :], ln_gb[k:k + 1, :].to_broadcast([P, H])).then_inc(weights_in, 16)
            sp.dma_start(b3[:, :], rows[0:1, 0:H].to_broadcast([P, H])).then_inc(weights_in, 16)
            sp.wait_ge(default_set, 5)
            for h in range(2):
                sp.dma_start(w1d[h * R:(h + 1) * R, h * R:(h + 1) * R], w1).then_inc(weights_in, 16)
            for s in range(3):
                sp.dma_start(rec_v[s], rec[0][:, 0:ST[s], :]).then_inc(default_out, 16)

            for c in (0, 1):
                sp.dma_start(xt_c[c], xT_v[c]).then_inc(xt_in[c], 16)
            for c in range(CHUNKS):
                sp.wait_ge(y_evac, 4 * c + 4)
                sp.dma_start(y_v[c], y_c[c % 2]).then_inc(y_out[c % 2], 16)
                if c + 2 < CHUNKS:
                    sp.dma_start(xt_c[c % 2], xT_v[c + 2]).then_inc(xt_in[c % 2], 16)
            for b in range(2):
                sp.wait_ge(y_out[b], 16 * slot_uses(CHUNKS, b))

            def load_part(s):
                for b in range(2):
                    sp.wait_ge(scattered[s][b], 16 * SU * slot_uses(UNITS[s], b))
                sp.dma_start(rec[0][:, TILE0[s]:TILE0[s] + ST[s], :], rec_v[s]).then_inc(rec_in[s], 16)
                sp.wait_ge(rows_evac, 4 * s + 4)
                full = ST[s] // P
                for f in range(2):
                    o = slot_rows[f, TILE0[s] * P:(TILE0[s] + ST[s]) * P]
                    sp.dma_start(o[0:full * P * P].rearrange("(j t l) -> t j l", t=P, l=P),
                                 rows_of_slots[:, f, 0:full, :]).then_inc(rows_out, 16)
                    sp.dma_start(o[full * P * P:ST[s] * P].rearrange("(t l) -> t l", l=P),
                                 rows_of_slots[0:ST[s] - full * P, f, full, :]).then_inc(rows_out, 16)
                sp.wait_ge(rows_out, 64 * s + 64)

            load_part(0)

            def load_de(g, q, b):
                if not (isinstance(g, int) and g < 2):
                    sp.wait_ge(rbf_done, g - 1)
                for f in range(2):
                    for h in range(2):
                        sp.dma_start(de[b][h * R:(h + 1) * R, f, :],
                                     slot_rows[f:f + 1, bass.ds(g * (GT * P) + h * GW, GW)].to_broadcast([R, GW])
                                     ).then_inc(de_in[b], 16)

            single(load_de, 0, 1, 2)
            pairs(sp, load_de, 3, GA - 2)
            single(load_de, GA - 1)
            load_part(1)
            single(load_de, GA)
            pairs(sp, load_de, GA + 1, G0 - 1)

            for b in range(2):
                sp.wait_ge(scattered[2][b], 16 * SU * slot_uses(UNITS[2], b))
            sp.dma_start(rec[1][:, :, :], rec_v[2]).then_inc(rec_in[2], 16)

            def x_load(c):
                if c >= 3:
                    sp.wait_ge(gated, c - 2)
                sp.dma_start(by_block(x_c[c % 3]), x_v[c]).then_inc(x_in[c % 3], 16)

            def x1_store(c):
                sp.wait_ge(x1_set, c + 1)
                for k in range(2):
                    sp.dma_start(x1_v[k][c], by_block(x1_c[c % 2])[:, :, k * HALF:(k + 1) * HALF]
                                 ).then_inc(x1_out[c % 2], 16)
                sp.dma_start(agg[:, c * CB * H:(c + 1) * CB * H], x1_c[c % 2]).then_inc(x1_out[c % 2], 16)

            for c in range(CHUNKS + 3):
                if c < CHUNKS:
                    x_load(c)
                if c >= 3:
                    x1_store(c - 3)

            with sp.Fori(0, CHUNKS) as c:
                sp.wait_ge(last_vector, c + 1)
                sp.wait_ge(last_scalar, c + 1)
                sp.dma_start(out_v[c], agg[:, bass.ds(c * (CB * H), CB * H)].rearrange("p (j n) -> p j n", j=CB)
                             ).then_inc(out_done, 16)
            sp.wait_ge(out_done, 16 * CHUNKS)

        @block.gpsimd
        def _(pool):
            nc.gpsimd.iota(lane[:, :], [[1, P]], base=0, channel_multiplier=0,
                           allow_small_or_imprecise_dtypes=True).then_inc(consts, 1)
            nc.gpsimd.iota(tile_no, [[1, TILES[0]]], base=0, channel_multiplier=0,
                           allow_small_or_imprecise_dtypes=True).then_inc(consts, 1)
            nc.gpsimd.memset(ones[:, :], 1.0).then_inc(consts, 1)
            nc.gpsimd.memset(ones3[:, :], 1.0).then_inc(consts, 1)
            pool.wait_ge(consts, 4)
            nc.gpsimd.affine_select(out=before[:, :], in_=ones[:, :], compare_op=ALU.is_gt, fill=0.0,
                                    base=0, pattern=[[1, P]], channel_multiplier=-1).then_inc(consts, 1)
            nc.gpsimd.affine_select(out=ident[:, :], in_=ones[:, :], compare_op=ALU.is_equal, fill=0.0,
                                    base=0, pattern=[[1, P]], channel_multiplier=-1).then_inc(consts, 1)

            nc.gpsimd.memset(agg[:, 2 * CB * H:], 0.0).then_inc(consts, 1)

            def scatter(s):
                def body(u, q, b):
                    hold(pool, sc_staged, 2 * u + 2 + 2 * sum(UNITS[:s]))
                    for t in range(SU):
                        pool.indirect_dma_start(
                            records[s], bass.IndirectOffsetOnAxis(ap=sc_adr[b][:, t:t + 1], axis=0),
                            sc_rec[b][:, t, :], None).then_inc(scattered[s][b], 16)
                return body

            def gather(g, q, b):
                hold(pool, idx_staged, g + 1)
                if not (isinstance(g, int) and g < 2):
                    hold(pool, msg_done, 2 * g - 2)
                for t in range(GT):
                    pool.indirect_dma_start(
                        gath[b][:, t, :], None, y_rows,
                        bass.IndirectOffsetOnAxis(ap=idx[b][:, t:t + 1], axis=0)).then_inc(gathered[b], 16)

            pool.wait_ge(default_out, 48)
            single(scatter(0), 0, 1, 2)
            pairs(pool, scatter(0), 3, UNITS[0] - 2)
            single(scatter(0), UNITS[0] - 1)
            single(scatter(1), 0, 1)

            def gather_scatter_src(g, q, b):
                gather(g, q, b)
                scatter(1)(g + 2, q + 1, b)

            def gather_scatter_dst(g, q, b):
                gather(g, q, b)
                scatter(2)(g - GA, q - GA // 2, b)

            for b in range(2):
                pool.wait_ge(y_out[b], 16 * slot_uses(CHUNKS, b))
            single(gather_scatter_src, 0, 1, 2)
            pairs(pool, gather_scatter_src, 3, GB - 1)
            single(gather, *range(GB, GA))
            single(gather_scatter_dst, GA, GA + 1, GA + 2)
            pairs(pool, gather_scatter_dst, GA + 3, GA + UNITS[2] - 1)
            single(gather, GA + UNITS[2], GA + UNITS[2] + 1)
            pairs(pool, gather, GA + UNITS[2] + 2, G0 - 3)
            single(gather, G0 - 2, G0 - 1)

            for c in range(CHUNKS):
                h = by_block(h_c[c % 3])
                pool.wait_ge(affine, c + 1)
                nc.gpsimd.tensor_tensor(h, h, gb[:, 0:1, :].to_broadcast([P, CB, H]), ALU.mult).then_inc(gained, 1)
                pool.wait_ge(gained, c + 1)
                nc.gpsimd.tensor_tensor(h, h, gb[:, 1:2, :].to_broadcast([P, CB, H]), ALU.add).then_inc(normed, 1)

            for b in range(2):
                pool.wait_ge(x1_out[b], 48 * slot_uses(CHUNKS, b))
            for k in range(2):
                def gather2(g, q, b):
                    hold(pool, idx2_staged[k], g + 1)
                    if not (isinstance(g, int) and g < 2):
                        hold(pool, scaled[k], g - 1)
                    for t in range(GT):
                        pool.indirect_dma_start(
                            gath[b][:, t, 0:HALF], None, x1_half[k],
                            bass.IndirectOffsetOnAxis(ap=idx[b][:, t:t + 1], axis=0)).then_inc(gathered2[k][b], 16)
                if k:
                    hold(pool, scaled[0], G0)
                all_groups(pool, gather2, GROUPS[k])

        @block.scalar
        def _(act):
            act.wait_ge(envelope, 1)
            nc.scalar.activation(run, eq, ACT.Sin).then_inc(envelope, 1)

            def y_evacuate(c, q, b):
                if not isinstance(c, int) or c >= 2:
                    act.wait_ge(y_out[b], 16 * q)
                for j in range(4):
                    w = 2 if j < 3 else 1
                    act.wait_ge(y_mm, 4 * c + j + 1)
                    nc.scalar.activation(y_c[b][:, 2 * j:2 * j + w, :].rearrange("p a b -> p (a b)"),
                                         ps[:, j, 0:w * H], ACT.Copy).then_inc(y_evac, 1)

            single(y_evacuate, 0, 1, 2)
            pairs(act, y_evacuate, 3, CHUNKS - 1)

            def stage(s):
                def body(u, q, b):
                    if not isinstance(u, int) or u >= 2:
                        hold(act, scattered[s][b], 16 * SU * q)
                    elif s:
                        hold(act, scattered[s - 1][b], 16 * SU * slot_uses(UNITS[s - 1], b))
                    nc.scalar.activation(sc_rec[b][:, :, :].rearrange("p a b -> p (a b)"),
                                         stage_rec[s // 2][:, bass.ds(u * (4 * SU) + 4 * COL0[s], 4 * SU)],
                                         ACT.Copy).then_inc(sc_staged, 1)
                    nc.scalar.activation(sc_adr[b][:, :], stage_adr[s // 2][:, bass.ds(u * SU + COL0[s], SU)],
                                         ACT.Copy).then_inc(sc_staged, 1)
                return body

            act.wait_ge(sorted_key, 1)
            single(stage(0), 0, 1, 2)
            pairs(act, stage(0), 3, UNITS[0] // 2 - 2)
            single(stage(0), UNITS[0] // 2 - 1)
            act.wait_ge(sorted_key, 2)
            single(stage(0), UNITS[0] // 2)
            pairs(act, stage(0), UNITS[0] // 2 + 1, UNITS[0] - 2)
            single(stage(0), UNITS[0] - 1)
            act.wait_ge(sorted_key, 3)
            single(stage(1), 0, 1)

            def evacuate_rows(s):
                act.wait_ge(rows_mm, s + 1)
                if s:
                    act.wait_ge(rows_out, 64)
                full = ST[s] // P
                for f, j, w, bank, c in row_blocks(s):
                    if j == full - 1:
                        nc.scalar.activation(rows_of_slots[:, f, 0:full, :].rearrange("p a b -> p (a b)"),
                                             ps[:, bank, 0:full * P], ACT.Copy).then_inc(rows_evac, 1)
                    if j == full:
                        nc.scalar.activation(rows_of_slots[0:w, f, j, :], ps[0:w, bank, c:c + P],
                                             ACT.Copy).then_inc(rows_evac, 1)

            act.wait_ge(table_set, 3)
            evacuate_rows(0)

            def radial(g, q, b):
                act.wait_ge(de_in[b], 64 * q + 64)
                if not (isinstance(g, int) and g == 0):
                    act.wait_ge(tanh_done, g)
                nc.scalar.activation(sq, de[b][:, 0, :], ACT.Square, bias=negc[:, 0:1]).then_inc(squared, 1)
                act.wait_ge(squared, g + 1)
                nc.scalar.activation(th[b], sq, ACT.Tanh, scale=zscale[:, 0:1]).then_inc(tanh_done, 1)

            def silu1(g, q, b):
                act.wait_ge(l1_mm, g + 1)
                nc.scalar.activation(s1[b], ps[:, 0, 0:GW], ACT.Silu,
                                     bias=col[:, 2:3]).then_inc(s1_done, 1)

            def silu2(g):
                act.wait_ge(l23_mm, g + 1)
                for m in range(2):
                    nc.scalar.activation(s2[:, m, :].rearrange("p (h e) -> p h e", h=2),
                                         ps[:, 1:3, m * GW:(m + 1) * GW], ACT.Silu,
                                         bias=b23[:, m:m + 1]).then_inc(s2_done, 1)

            def silu3(g):
                for m in range(2):
                    act.wait_ge(l4_mm, 2 * g + m + 1)
                    nc.scalar.activation(s3[:, m, :], ps[:, 3 + m, :], ACT.Silu,
                                         bias=col[:, 5 + m:6 + m]).then_inc(s3_done, 1)

            def stage_idx(g, q, b):
                if not (isinstance(g, int) and g < 2):
                    hold(act, gathered[b], 16 * GT * q)
                nc.scalar.activation(idx[b][:, :], rec[0][:, bass.ds(g * GT, GT), 1],
                                     ACT.Copy).then_inc(idx_staged, 1)

            def act_group(scatters, ahead=2):
                def body(g, q, b):
                    silu2(g)
                    if ahead == 2:
                        radial(g + 2, q + 1, b)
                    if ahead:
                        stage_idx(g + 1, q + b, 1 - b)
                    if scatters == 1:
                        stage(1)(g + 2, q + 1, b)
                    if scatters == 2:
                        stage(2)(g - GA, q - GA // 2, b)
                    silu3(g)
                    if ahead:
                        silu1(g + 1, q + b, 1 - b)
                return body

            act.wait_ge(weights_in, 16 * n_weights)
            act.wait_ge(params_set, 2)
            act.wait_ge(rec_in[0], 16)
            radial(0, 0, 0)
            radial(1, 0, 1)
            stage_idx(0, 0, 0)
            silu1(0, 0, 0)
            single(act_group(1), 0, 1, 2)
            pairs(act, act_group(1), 3, GB - 1)
            single(act_group(0), GB)
            evacuate_rows(1)
            act.wait_ge(rec_in[1], 16)
            single(act_group(0), *range(GB + 1, GA))
            act.wait_ge(sorted_key, 4)
            single(act_group(2), GA, GA + 1, GA + 2)
            pairs(act, act_group(2), GA + 3, GA + UNITS[2] - 1)
            single(act_group(0), GA + UNITS[2], GA + UNITS[2] + 1)
            pairs(act, act_group(0), GA + UNITS[2] + 2, G0 - 3)
            single(act_group(0, 1), G0 - 2)
            single(act_group(0, 0), G0 - 1)

            def std1_step(c):
                act.wait_ge(var1_set, c + 1)
                nc.scalar.activation(std1[:, :], var_eps1[:, :], ACT.Sqrt).then_inc(std1_set, 1)

            def transposes_out(c):
                for j in range(4):
                    w = 4 * P if j < 3 else 2 * P
                    act.wait_ge(tr_mm, 4 * c + j + 1)
                    nc.scalar.activation(tr_c[:, j * 4 * P:j * 4 * P + w], ps[:, j, 0:w],
                                         ACT.Copy).then_inc(tr_evac, 1)

            def gates_out(c):
                if c:
                    act.wait_ge(gated, c)
                for j in range(4):
                    w = 2 * H if j < 3 else H
                    act.wait_ge(gate_mm, 4 * c + j + 1)
                    nc.scalar.activation(gate_c[:, j * 2 * H:j * 2 * H + w], ps[:, 4 + j, 0:w],
                                         ACT.Tanh, scale=0.5).then_inc(gate_evac, 1)

            def std2_step(c):
                act.wait_ge(var2_set, c + 1)
                nc.scalar.activation(std[:, :], var_eps[:, :], ACT.Sqrt).then_inc(std2_set, 1)

            def normalise1(c):
                act.wait_ge(rstd1_set, c + 1)
                b, h = c % 3, by_block(h_c[c % 3])
                for j in range(CB):
                    last = nc.scalar.activation(h[:, j, :], h[:, j, :], ACT.Identity,
                                                bias=shift1[b][:, j:j + 1], scale=rstd1[b][:, j:j + 1])
                last.then_inc(affine, 1)

            for c in (0, 1):
                std1_step(c)
                normalise1(c)
            for c in range(CHUNKS):
                transposes_out(c)
                if c + 2 < CHUNKS:
                    std1_step(c + 2)
                gates_out(c)
                if c + 2 < CHUNKS:
                    normalise1(c + 2)
                std2_step(c)

            act.wait_ge(rec_in[2], 16)
            for k in range(2):
                def stage_idx2(g, q, b):
                    if not isinstance(g, int) or g >= 2:
                        hold(act, gathered2[k][b], 16 * GT * q)
                    elif k:
                        hold(act, gathered2[0][b], 16 * GT * slot_uses(G0, b))
                    nc.scalar.activation(idx[b][:, :], rec[k][:, bass.ds(g * GT, GT), 1],
                                         ACT.Copy).then_inc(idx2_staged[k], 1)
                all_groups(act, stage_idx2, GROUPS[k])

            act.wait_ge(last_var, 1)
            nc.scalar.activation(last_sd, last_eps, ACT.Sqrt).then_inc(last_std, 1)
            act.wait_ge(last_rstd, 1)
            for c in range(CHUNKS):
                for j in range(c * CB + VB, (c + 1) * CB):
                    rows_of = agg[:, j * H:(j + 1) * H]
                    last = nc.scalar.activation(rows_of, rows_of, ACT.Identity, bias=last_shift[:, j:j + 1],
                                                scale=last_inv[:, j:j + 1])
                last.then_inc(last_scalar, 1)

        @block.tensor
        def _(pe):
            mm = nc.tensor.matmul
            pe.wait_ge(weights_in, 16 * n_weights)
            pe.wait_ge(consts, 6)
            mm(ps[:, 4, 0:H], w2t[:, :], f1s[:, :], start=True, stop=True)
            for m in range(2):
                last = mm(ps[:, 5, m:m + 1], f1s[:, m * P:(m + 1) * P], col[0:R, 7:8], start=True, stop=True)
            last.then_inc(fused_mm, 1)
            pe.wait_ge(biases_set, 1)

            def y_product(c, q, b):
                pe.wait_ge(xt_in[b], 16 * q + 16)
                for j in range(CB):
                    if j % 2 == 0 and not (isinstance(c, int) and c == 0):
                        pe.wait_ge(y_evac, 4 * c + j // 2 - 3)
                    o = ps[:, j // 2, (j % 2) * H:(j % 2 + 1) * H]
                    for k in range(2):
                        mm(o, xt_c[b][:, k, j * P:(j + 1) * P], nws[:, k, :], start=(k == 0), stop=False)
                    last = mm(o, ones3[:, :], bias3[:, 1, :], start=False, stop=True)
                    if j % 2 or j == CB - 1:
                        last.then_inc(y_mm, 1)

            def prefix(s):
                pe.wait_ge(counted, s + 1)
                mm(ps[:, 6, 0:NB], before[:, :], cnt[:, 0:NB], start=True, stop=True)
                mm(ps[:, 6, 64:64 + NB], ones[:, :], cnt[:, 0:NB], start=True, stop=True)
                mm(ps[0:NB, 6, 128:129], cnt[:, 0:NB], ones[:, 0:1], start=True, stop=True).then_inc(prefix_mm, 1)
                pe.wait_ge(tiles_set, s + 1)
                mm(ps[0:NB, 6, 130:131], before[0:NB, 0:NB], ntc[:, :], start=True, stop=True).then_inc(starts_mm, 1)
                pe.wait_ge(reached_set, s + 1)
                for bank, lo, hi in table_parts(s):
                    last = mm(ps[:, bank, 0:hi - lo], ones[0:NB, :], reached[:, lo:hi], start=True, stop=True)
                last.then_inc(table_mm, 1)
                pe.wait_ge(table_set, s + 1)

            single(y_product, 0, 1, 2)
            prefix(0)
            pairs(pe, y_product, 3, CHUNKS - 1)
            prefix(1)
            prefix(2)

            def part_rows(s):
                pe.wait_ge(rec_in[s], 16)
                for f, j, w, bank, c in row_blocks(s):
                    at = TILE0[s] + j * P
                    last = nc.tensor.transpose(ps[0:w, bank, c:c + P], rec[0][:, at:at + w, 2 + f], ident[:, :])
                last.then_inc(rows_mm, 1)
                pe.wait_ge(rows_evac, 4 * s + 4)

            part_rows(0)

            def layer1(g, q, b):
                pe.wait_ge(rbf_done, g + 1)
                if not (isinstance(g, int) and g < 3):
                    pe.wait_ge(added, 4 * g - 8)
                mm(ps[:, 0, 0:GW], w1d[:, :], rbf[b], start=True, stop=True).then_inc(l1_mm, 1)

            def layer23(g, q, b):
                pe.wait_ge(s1_done, g + 1)
                for m in range(2):
                    for h in range(2):
                        last = mm(ps[:, 1 + h, m * GW:(m + 1) * GW],
                                  w23[h * R:(h + 1) * R, m * P:(m + 1) * P],
                                  s1[b][h * R:(h + 1) * R, :], start=True, stop=True)
                last.then_inc(l23_mm, 1)

            def layer4(g):
                pe.wait_ge(s2_done, 2 * g + 2)
                for m in range(2):
                    for k in range(2):
                        last = mm(ps[:, 3 + m, :], f2s[:, k, m * P:(m + 1) * P], s2[:, k, :],
                                  start=(k == 0), stop=(k == 1))
                    last.then_inc(l4_mm, 1)

            def layer5(g):
                pe.wait_ge(s3_done, 2 * g + 2)
                for t in range(GT):
                    if t % 2 == 0 and not (isinstance(g, int) and g < 1):
                        pe.wait_ge(biased, 2 * g + t // 2 - 1)
                    o = ps[:, 5 + t // 2, (t % 2) * H:(t % 2 + 1) * H]
                    for k in range(2):
                        last = mm(o, s3[:, k, t * P:(t + 1) * P], f3s[:, k, :], start=(k == 0), stop=(k == 1))
                    if t % 2:
                        last.then_inc(l5_mm, 1)

            def aggregate(g, b):
                pe.wait_ge(hot_done, g + 1)
                for h in range(2):
                    pe.wait_ge(msg_done, 2 * g + h + 1)
                    if not (isinstance(g, int) and g == 0):
                        pe.wait_ge(added, 4 * g - 2 + 2 * h)
                    if h:
                        pe.wait_ge(s1_done, min(g + 3, G0) if isinstance(g, int) else g + 3)
                    for t in (2 * h, 2 * h + 1):
                        last = mm(ps[:, 7 * (1 - h), (t % 2) * H:(t % 2 + 1) * H], hot[b][:, t, :], msg[:, t, :],
                                  start=True, stop=True)
                    last.then_inc(agg_mm, 1)

            def pe_group(g, q, b, before_it=True, after_it=True):
                layer23(g, q, b)
                if before_it:
                    layer5(g - 1)
                layer4(g)
                if after_it:
                    layer1(g + 1, q + b, 1 - b)
                if before_it:
                    aggregate(g - 1, 1 - b)

            layer1(0, 0, 0)
            pe_group(0, 0, 0, before_it=False)
            single(pe_group, 1, 2)
            pairs(pe, pe_group, 3, GB - 1)
            single(pe_group, GB)
            pe.wait_ge(msg_done, 2 * GB)
            pe.wait_ge(added, GT * GB)
            part_rows(1)
            single(pe_group, GB + 1)
            pairs(pe, pe_group, GB + 2, G0 - 3)
            single(pe_group, G0 - 2)
            pe_group(G0 - 1, G0 // 2, 0, after_it=False)
            layer5(G0 - 1)
            aggregate(G0 - 1, 0)

            def node_products(c):
                first = c == 0
                pe.wait_ge(normed, c + 1)
                for j in range(2 * CB):
                    if j % 4 == 0 and not first:
                        pe.wait_ge(tr_evac, 4 * c + j // 4 - 3)
                    last = nc.tensor.transpose(ps[:, j // 4, (j % 4) * P:(j % 4 + 1) * P],
                                               h_c[c % 3][:, j * P:(j + 1) * P], ident[:, :])
                    if j % 4 == 3 or j == 2 * CB - 1:
                        last.then_inc(tr_mm, 1)
                for j in range(CB):
                    if j % 2 == 0:
                        pe.wait_ge(tr_evac, 4 * c + j // 2 + 1)
                        if not first:
                            pe.wait_ge(gate_evac, 4 * c + j // 2 - 3)
                    o = ps[:, 4 + j // 2, (j % 2) * H:(j % 2 + 1) * H]
                    for k in range(2):
                        mm(o, tr_c[:, (2 * j + k) * P:(2 * j + k + 1) * P], gws[:, k, :],
                           start=(k == 0), stop=False)
                    last = mm(o, ones3[:, :], bias3[:, 2, :], start=False, stop=True)
                    if j % 2 or j == CB - 1:
                        last.then_inc(gate_mm, 1)

            for c in range(CHUNKS):
                node_products(c)

            for k in range(2):
                def aggregate2(g, q, b):
                    pe.wait_ge(hot2_done[k], g + 1)
                    pe.wait_ge(scaled[k], g + 1)
                    if not (isinstance(g, int) and g < 2):
                        pe.wait_ge(added2[k], GT * (g - 1))
                    for t in range(GT):
                        last = mm(ps[:, 2 * b + t // 2, (t % 2) * H:(t % 2) * H + ACW], hot[b][:, t, :],
                                  msg2[b][:, t, :], start=True, stop=True)
                        if t % 2:
                            last.then_inc(agg2_mm[k], 1)
                if k:
                    pe.wait_ge(added2[0], GT * G0)
                all_groups(pe, aggregate2, GROUPS[k])

        @block.vector
        def _(dve):
            V = nc.vector

            def stepper(s, start=0):
                n = [0]

                def step(ins):
                    n[0] += 1
                    ins.then_inc(s, 1)
                    dve.wait_ge(s, start + n[0])
                step.count = n
                return step


            for f, v in enumerate((-1.0, float(PAD_NODE), 0.0, 0.0)):
                V.memset(rec[0][:, 0:max(ST), f], v).then_inc(default_set, 1)
            V.memset(w1d[:, :], 0.0).then_inc(default_set, 1)
            V.memset(offs[:, NB:NB2], 0.0)

            step = stepper(chain)
            dve.wait_ge(edges_in, 48)
            step(V.tensor_scalar(run, wt, 0.5 / CUTOFF, None, ALU.mult))
            step(V.scalar_tensor_tensor(eq, run, -1.0, run, ALU.mult, ALU.max))
            step(V.tensor_scalar(run, eq, ROUND, None, ALU.add))
            step(V.tensor_scalar(run, run, -ROUND, None, ALU.add))
            step(V.tensor_tensor(eq, eq, run, ALU.subtract))
            step(V.scalar_tensor_tensor(run, eq, -1.0, eq, ALU.mult, ALU.max))
            V.tensor_scalar(eq, run, -2.0 * math.pi, 0.5 * math.pi, ALU.mult, ALU.add).then_inc(envelope, 1)
            step(V.tensor_scalar(blk, wt, CUTOFF, None, ALU.is_lt))
            srec = [t.rearrange("p (e f) -> p e f", f=4) for t in stage_rec]
            dve.wait_ge(envelope, 2)
            step(V.scalar_tensor_tensor(srec[0][:, :, 3], run, 1.0, blk, ALU.add, ALU.mult))
            V.memset(srec[1][:, :, 3], 0.0)

            def prepare(k):
                step(V.tensor_scalar(eq.bitcast(i32), key_i[k], 7, None, ALU.logical_shift_right))
                step(V.tensor_copy(blk, eq.bitcast(i32)))
                step(V.tensor_scalar(run.bitcast(i32), key_i[k], P - 1, None, ALU.bitwise_and))
                V.tensor_copy(srec[k][:, :, 0], run.bitcast(i32))
                V.tensor_copy(srec[k][:, :, 1], key_i[1 - k])
                step(V.tensor_copy(srec[k][:, :, 2], wt))

            def columns(s, t):
                return t[:, COL0[s]:COL0[s] + COLS[s]]

            def count(s):
                done = step.count[0]
                with dve.Fori(0, NB2 // 2) as i:
                    for j, scratch in enumerate((eq, run)):
                        dve.wait_ge(chain, done + 2 * i + (j - 1))
                        V.tensor_scalar(columns(s, scratch), columns(s, blk), lane[:, bass.ds(2 * i + j, 1)],
                                        None, ALU.is_equal, ALU.add,
                                        accum_out=cnt[:, bass.ds(2 * i + j, 1)]).then_inc(chain, 1)
                step.count[0] += NB2
                dve.wait_ge(chain, step.count[0])
                V.memset(columns(s, rank), 0.0).then_inc(counted, 1)
                dve.wait_ge(prefix_mm, s + 1)
                step(V.tensor_scalar(nt_i[:, :], ps[:, 6, 64:64 + NB], float(P - 1), None, ALU.add))
                step(V.tensor_scalar(nt_i[:, :], nt_i[:, :], 7, None, ALU.logical_shift_right))
                step(V.tensor_copy(tot[:, :], nt_i[:, :]))
                step(V.tensor_tensor_scan(start[:, :], tot[:, :], tot[:, :], 0.0, ALU.add, ALU.max))
                step(V.tensor_tensor(start[:, :], start[:, :], tot[:, :], ALU.subtract))
                step(V.scalar_tensor_tensor(offs[:, 0:NB], start[:, :], float(P), ps[:, 6, 0:NB], ALU.mult, ALU.add))
                step(V.tensor_scalar(ntc_i[:, :], ps[0:NB, 6, 128:129], float(P - 1), None, ALU.add))
                step(V.tensor_scalar(ntc_i[:, :], ntc_i[:, :], 7, None, ALU.logical_shift_right))
                V.tensor_copy(ntc[:, :], ntc_i[:, :]).then_inc(tiles_set, 1)
                dve.wait_ge(starts_mm, s + 1)
                step(V.tensor_copy(startc[:, :], ps[0:NB, 6, 130:131]))
                V.tensor_scalar(reached[:, 0:ST[s]], tile_no[0:NB, 0:ST[s]], startc[:, 0:1], None,
                                ALU.is_ge).then_inc(reached_set, 1)
                dve.wait_ge(table_mm, s + 1)
                for row, width in (((0, H), (1, ACW)) if s < 2 else ((2, ACW),)):
                    p = TROW[row]
                    for bank, lo, hi in table_parts(s):
                        last = V.tensor_scalar(table[p:p + 1, TILE0[s] + lo:TILE0[s] + hi],
                                               ps[p:p + 1, bank, 0:hi - lo], -1.0, float(width),
                                               ALU.add, ALU.mult)
                last.then_inc(table_set, 1)
                dve.wait_ge(table_set, s + 1)

            def ranks(s, lo, hi, carry=False):
                own, extra = slice(COL0[s] + lo, COL0[s] + hi), slice(lo, hi)
                sets = [[t[:, own] for t in (eq, run, rank)], [t[:, extra] for t in (eq1, run1, rank1)]]
                step(V.memset(sets[1][2], 0.0))
                done = step.count[0]
                turn = 2 * (5 if carry else 4)
                with dve.Fori(0, NB2 // 2) as i:
                    at = [0]

                    def do(make):
                        for j, (e, r, a) in enumerate(sets):
                            n = at[0] + j
                            dve.wait_ge(chain, done + turn * i + (n - 3 if n < 2 else n - 1))
                            make(e, r, a, bass.ds(2 * i + j, 1)).then_inc(chain, 1)
                        at[0] += 2

                    do(lambda e, r, a, b: V.tensor_scalar(e, blk[:, own], lane[:, b], None, ALU.is_equal))
                    do(lambda e, r, a, b: V.tensor_tensor_scan(r, e, e, offs[:, b], ALU.add, ALU.max))
                    if carry:
                        do(lambda e, r, a, b: V.tensor_tensor(offs[:, b], r[:, hi - lo - 1:hi - lo],
                                                              r[:, hi - lo - 1:hi - lo], ALU.max))
                    do(lambda e, r, a, b: V.tensor_tensor(r, r, e, ALU.mult))
                    do(lambda e, r, a, b: V.tensor_tensor(a, a, r, ALU.add))
                step.count[0] += turn * (NB2 // 2)
                dve.wait_ge(chain, step.count[0])

            def addresses(step, s, lo, hi, second_rank=None):
                own = slice(COL0[s] + lo, COL0[s] + hi)
                slot_i, lane_i, tile_i = (t[:, own].bitcast(i32) for t in (eq, run, blk))
                if second_rank is None:
                    step(V.tensor_scalar(slot_i, rank[:, own], -1.0, None, ALU.add))
                else:
                    step(V.scalar_tensor_tensor(slot_i, rank[:, own], -1.0, second_rank[:, lo:hi], ALU.add, ALU.add))
                step(V.tensor_scalar(lane_i, slot_i, P - 1, None, ALU.bitwise_and))
                step(V.tensor_scalar(tile_i, slot_i, 7, None, ALU.logical_shift_right))
                V.scalar_tensor_tensor(stage_adr[s // 2][:, own], lane_i, float(ST[s]), tile_i,
                                       ALU.mult, ALU.add).then_inc(sorted_key, 1)

            dve.wait_ge(consts, 6)
            dve.wait_ge(weights_in, 16 * n_weights)
            V.tensor_scalar(negc[:, :], col[:, 0:1], -1.0, None, ALU.mult)
            step(V.scalar_tensor_tensor(zscale[:, :], col[:, 1:2], -1.0, col[:, 1:2], ALU.mult, ALU.max))
            step(V.tensor_scalar(zscale[:, :], zscale[:, :], EPS_W, None, ALU.add))
            step(V.reciprocal(zscale[:, :], zscale[:, :]))
            step(V.tensor_tensor(zscale[:, :], zscale[:, :], zscale[:, :], ALU.mult))
            V.tensor_scalar(zscale[:, :], zscale[:, :], 0.25, None, ALU.mult).then_inc(params_set, 1)
            dve.wait_ge(fused_mm, 1)
            V.tensor_copy(w23[:, :], ps[:, 4, 0:H])
            V.tensor_tensor(b23[:, :], ps[:, 5, 0:2], col[:, 3:5], ALU.add).then_inc(params_set, 1)
            step(V.tensor_copy(part[0][:, :], r3[:, :]))
            step(V.tensor_tensor(r3b[0][:, :], r3[:, :], part[0][:, :], ALU.subtract))
            step(V.tensor_copy(part[1][:, :], r3b[0][:, :]))
            step(V.tensor_tensor(r3b[1][:, :], r3b[0][:, :], part[1][:, :], ALU.subtract))
            step(V.tensor_copy(part[2][:, :], r3b[1][:, :]))
            step(V.tensor_scalar(r3b[0][:, :], part[0][:, :], ident[0:3, 0:1], None, ALU.mult))
            for k in (1, 2):
                o = r3b[1][:, :] if k == 1 else bias3[:, :, :].rearrange("p a b -> p (a b)")
                i = r3b[0][:, :] if k == 1 else r3b[1][:, :]
                last = V.scalar_tensor_tensor(o, part[k][:, :], ident[0:3, k:k + 1], i, ALU.mult, ALU.add)
                if k == 1:
                    step(last)
            last.then_inc(biases_set, 1)

            prepare(0)
            count(0)
            for lo in (0, CA // 2):
                ranks(0, lo, lo + CA // 2, carry=(lo == 0))
                addresses(step, 0, lo, lo + CA // 2, rank1)
            dve.wait_ge(sorted_key, 2)
            count(1)
            ranks(1, 0, COLS[1])
            addresses(step, 1, 0, COLS[1], rank1)
            dve.wait_ge(sorted_key, 3)
            prepare(1)
            count(2)
            dve.sem_inc(rank_chain)
            for b in range(2):
                dve.wait_ge(y_out[b], 16 * slot_uses(CHUNKS, b))
            V.memset(agg[:, 0:2 * CB * H], 0.0)

            def rank_turn(at, n):
                dve.wait_ge(rank_chain, 4 * at + n + 1)
                ins = (V.tensor_scalar(eq, blk, lane[:, bass.ds(at, 1)], None, ALU.is_equal) if n == 0 else
                       V.tensor_tensor_scan(run, eq, eq, offs[:, bass.ds(at, 1)], ALU.add, ALU.max) if n == 1 else
                       V.tensor_tensor(run, run, eq, ALU.mult) if n == 2 else
                       V.tensor_tensor(rank, rank, run, ALU.add))
                ins.then_inc(rank_chain, 1)

            with dve.Fori(0, BR) as b:
                for n in range(4):
                    rank_turn(b, n)
            dve.wait_ge(rec_in[0], 16)
            dve.wait_ge(consts, 7)

            def radial_basis(g, q, b):
                dve.wait_ge(tanh_done, g + 1)
                V.tensor_scalar(up1, th[b], 1.0, None, ALU.add).then_inc(rbf_chain, 1)
                dve.wait_ge(rbf_chain, 2 * g + 1)
                if not (isinstance(g, int) and g == 0):
                    dve.wait_ge(rbf_done, g)
                V.reciprocal(rcp, up1).then_inc(rbf_chain, 1)
                dve.wait_ge(rbf_chain, 2 * g + 2)
                if not (isinstance(g, int) and g < 2):
                    dve.wait_ge(l1_mm, g - 1)
                V.scalar_tensor_tensor(rbf[b], rcp, -0.5, de[b][:, 1, :], ALU.add, ALU.mult).then_inc(rbf_done, 1)

            def one_hot(k, g, b, s):
                V.tensor_tensor(hot[b][:, :, :], lane[:, None, :].to_broadcast([P, GT, P]),
                                rec[k][:, bass.ds(g * GT, GT), 0:1].to_broadcast([P, GT, P]),
                                ALU.is_equal).then_inc(s, 1)

            def messages(g, q, b):
                dve.wait_ge(gathered[b], 16 * GT * q + 16 * GT)
                for h in range(2):
                    dve.wait_ge(l5_mm, 2 * g + h + 1)
                    m = msg[:, 2 * h:2 * h + 2, :]
                    V.tensor_tensor(m, ps[:, 5 + h, :].rearrange("p (a b) -> p a b", a=2),
                                    b3[:, None, :].to_broadcast([P, 2, H]), ALU.add).then_inc(biased, 1)
                    dve.wait_ge(biased, 2 * g + h + 1)
                    V.tensor_tensor(m, m, gath[b][:, 2 * h:2 * h + 2, :], ALU.mult).then_inc(msg_done, 1)

            def places_of(row, width, g):
                return nc.values_load_multi_w_load_instructions(
                    table[TROW[row]:TROW[row] + 1, bass.ds(g * GT, GT)], [mybir.EngineType.DVE],
                    min_val=0, max_val=(NB - 1) * width,
                    skip_runtime_bounds_check_because="a count of at most NB block starts, less one, and the "
                                                      "first block starts at tile 0")[1]

            def add_up(g):
                places = places_of(0, H, g)
                for t in range(GT):
                    if not (isinstance(g, int) and g == 0 and t == 0):
                        dve.wait_ge(added, GT * g + t)
                    dve.wait_ge(agg_mm, 2 * g + t // 2 + 1)
                    rows_of = agg[:, bass.ds(places[t], H)]
                    V.tensor_tensor(rows_of, rows_of, ps[:, 7 * (1 - t // 2), (t % 2) * H:(t % 2 + 1) * H],
                                    ALU.add).then_inc(added, 1)

            def dve_group(ahead=True, before_it=True, ranking=False):
                def body(g, q, b):
                    if ranking:
                        for n in (0, 1):
                            rank_turn(q - 2 + b + BR, 2 * (1 - b) + n)
                    one_hot(0, g, b, hot_done)
                    if ahead:
                        radial_basis(g + 2, q + 1, b)
                    if before_it:
                        messages(g - 1, q + b - 1, 1 - b)
                        add_up(g - 1)
                return body

            radial_basis(0, 0, 0)
            radial_basis(1, 0, 1)
            single(dve_group(before_it=False), 0)
            single(dve_group(), 1, 2)
            last_ranks = GR + 2 * (NB - BR) - 1
            pairs(dve, dve_group(ranking=True), GR, last_ranks)
            dve.wait_ge(rank_chain, 4 * NB + 1)
            addresses(stepper(rank_chain, 4 * NB + 1), 2, 0, EC)
            pairs(dve, dve_group(), last_ranks + 1, G0 - 3)
            single(dve_group(ahead=False), G0 - 2, G0 - 1)
            messages(G0 - 1, G0 // 2, 0)
            add_up(G0 - 1)

            for b in range(2):
                dve.wait_ge(scattered[2][b], 16 * SU * slot_uses(UNITS[2], b))

            def moments(step, src, mv=mv, var_eps=var_eps, done=None):
                for j in range(CB):
                    last = V.bn_stats(stats[:, j, :], by_block(src)[:, j, :])
                step(last)
                dve.sem_inc(carrier)
                for j in range(CB):
                    last = V.bn_aggr(mv[:, j, :], stats[:, j, :])
                step(last)
                last = V.tensor_scalar(var_eps[:, :], mv[:, :, 1], EPS_LN, None, ALU.add)
                if done is None:
                    step(last)
                else:
                    last.then_inc(done, 1)

            def normalise(step, dst, src, done=None):
                step(V.reciprocal(rstd[:, :], std[:, :]))
                for j in range(CB):
                    last = V.tensor_scalar(by_block(dst)[:, j, :], by_block(src)[:, j, :], mv[:, j, 0:1],
                                           rstd[:, j:j + 1], ALU.subtract, ALU.mult)
                if done is None:
                    step(last)
                else:
                    last.then_inc(done, 1)

            def residual(c):
                b = c % 3
                dve.wait_ge(x_in[b], 16 * (c // 3) + 16)
                if c >= 3:
                    dve.wait_ge(gated, c - 2)
                step(V.tensor_tensor(h_c[b], x_c[b], agg[:, c * CB * H:(c + 1) * CB * H], ALU.add))
                moments(step, h_c[b], mv1[b], var_eps1, var1_set)

            def reciprocal1(c):
                b = c % 3
                dve.wait_ge(std1_set, c + 1)
                step(V.reciprocal(rstd1[b][:, :], std1[:, :]))
                V.scalar_tensor_tensor(shift1[b][:, :], mv1[b][:, :, 0], -1.0, rstd1[b][:, :],
                                       ALU.mult, ALU.mult).then_inc(rstd1_set, 1)

            def gate(c):
                dve.wait_ge(normed, c + 1)
                dve.wait_ge(gate_evac, 4 * c + 4)
                step(V.scalar_tensor_tensor(gate_c, gate_c, 1.0, h_c[c % 3], ALU.add, ALU.mult))
                if c:
                    dve.wait_ge(x1_set, c)
                V.scalar_tensor_tensor(res_c, gate_c, 0.5, x_c[c % 3], ALU.mult, ALU.add).then_inc(gated, 1)
                dve.wait_ge(gated, c + 1)
                moments(step, res_c, done=var2_set)

            def finish(c):
                dve.wait_ge(std2_set, c + 1)
                if c >= 2:
                    dve.wait_ge(x1_out[c % 2], 48 * (c // 2))
                normalise(step, x1_c[c % 2], res_c, done=x1_set)

            step = stepper(nv)
            for c in (0, 1):
                residual(c)
                reciprocal1(c)
            for c in range(CHUNKS):
                if c + 2 < CHUNKS:
                    residual(c + 2)
                if c:
                    finish(c - 1)
                if c + 2 < CHUNKS:
                    reciprocal1(c + 2)
                gate(c)
            finish(CHUNKS - 1)
            for b in range(2):
                dve.wait_ge(x1_out[b], 48 * slot_uses(CHUNKS, b))
            for k in range(2):
                V.memset(msg2[k][:, :, HALF:ACW], 1.0)
            V.memset(acc[0], 0.0)
            dve.wait_ge(rec_in[2], 16)

            step = stepper(mean_steps)

            def degrees(k):
                deg = acc[k].rearrange("p (n f) -> p n f", f=ACW)[:, :, HALF]
                step(V.tensor_scalar(rdeg[k][:, :], deg, 1.0, None, ALU.max))
                step(V.reciprocal(rdeg[k][:, :], rdeg[k][:, :]))

            def merge(k, n):
                rows_of = agg[:, bass.ds(n * H + k * HALF, HALF)]
                V.scalar_tensor_tensor(rows_of, acc[k][:, bass.ds(n * ACW, HALF)], rdeg[k][:, bass.ds(n, 1)],
                                       rows_of, ALU.mult, ALU.add).then_inc(merged, 1)
                dve.wait_ge(merged, 2 * n + 1 + 2 * NB * k)
                V.bn_stats(half_stats[:, bass.ds(n, 1), k, :], rows_of).then_inc(merged, 1)

            for k in range(2):
                def scale(g, q, b):
                    dve.wait_ge(gathered2[k][b], 16 * GT * q + 16 * GT)
                    V.tensor_tensor(msg2[b][:, :, 0:HALF], gath[b][:, :, 0:HALF],
                                    rec[k][:, bass.ds(g * GT, GT), 2:3].to_broadcast([P, GT, HALF]),
                                    ALU.mult).then_inc(scaled[k], 1)

                def sums(g, b):
                    places = places_of(1 + k, ACW, g)
                    for t in range(GT):
                        if not (isinstance(g, int) and g == 0 and t == 0):
                            dve.wait_ge(added2[k], GT * g + t)
                        dve.wait_ge(agg2_mm[k], 2 * g + t // 2 + 1)
                        rows_of = acc[k][:, bass.ds(places[t], ACW)]
                        V.tensor_tensor(rows_of, rows_of,
                                        ps[:, 2 * b + t // 2, (t % 2) * H:(t % 2) * H + ACW],
                                        ALU.add).then_inc(added2[k], 1)

                def group2(g, q, b):
                    one_hot(k, g, b, hot2_done[k])
                    scale(g, q, b)
                    if not (isinstance(g, int) and g == 0):
                        sums(g - 1, 1 - b)

                if k == 0:
                    single(group2, 0, 1, 2)
                    V.memset(acc[1], 0.0)
                    pairs(dve, group2, 3, G0 - 3)
                    single(group2, G0 - 2, G0 - 1)
                    sums(G0 - 1, 0)
                    dve.wait_ge(added2[0], GT * G0)
                    degrees(0)
                    continue

                def group2_merge(g, q, b):
                    group2(g, q, b)
                    merge(0, g - 3)

                single(group2, 0, 1, 2)
                pairs(dve, group2_merge, 3, NB + 1)
                single(group2_merge, NB + 2)
                single(group2, NB + 3)
                pairs(dve, group2, NB + 4, G1 - 3)
                single(group2, G1 - 2, G1 - 1)
                sums(G1 - 1, 0)
                dve.wait_ge(added2[1], GT * G1)
                degrees(1)

            for n in range(NB):
                V.scalar_tensor_tensor(agg[:, n * H + HALF:(n + 1) * H], acc[1][:, n * ACW:n * ACW + HALF],
                                       rdeg[1][:, n:n + 1], agg[:, n * H + HALF:(n + 1) * H],
                                       ALU.mult, ALU.add).then_inc(merged, 1)
                if n:
                    dve.wait_ge(merged, 2 * NB + n)
                    V.bn_stats(half_stats[:, n - 1, 1, :], agg[:, (n - 1) * H + HALF:n * H])
            dve.wait_ge(merged, 3 * NB)
            step(V.bn_stats(half_stats[:, NB - 1, 1, :], agg[:, (NB - 1) * H + HALF:NB * H]))
            for n in range(NB):
                last = V.bn_aggr(last_mv[:, n, :], half_stats[:, n, :, :])
            step(last)
            V.tensor_scalar(last_eps, last_mv[:, :, 1], EPS_LN, None, ALU.add).then_inc(last_var, 1)
            dve.wait_ge(last_std, 1)
            step(V.reciprocal(last_inv, last_sd))
            V.scalar_tensor_tensor(last_shift, last_mv[:, :, 0], -1.0, last_inv,
                                   ALU.mult, ALU.mult).then_inc(last_rstd, 1)
            for c in range(CHUNKS):
                for j in range(c * CB, c * CB + VB):
                    rows_of = agg[:, j * H:(j + 1) * H]
                    last = V.tensor_scalar(rows_of, rows_of, last_mv[:, j, 0:1], last_inv[:, j:j + 1],
                                           ALU.subtract, ALU.mult)
                last.then_inc(last_vector, 1)


def kernel(x, src, dst, edge_weight, L0_gnn_centers, L0_gnn_widths, L0_gnn_rbf_w1, L0_gnn_rbf_b1,
           L0_gnn_rbf_w2, L0_gnn_rbf_b2, L0_gnn_filt_w1, L0_gnn_filt_b1, L0_gnn_filt_w2, L0_gnn_filt_b2,
           L0_gnn_filt_w3, L0_gnn_filt_b3, L0_gnn_node_w, L0_gnn_node_b, L0_gnn_ln_g, L0_gnn_ln_b,
           L0_gnn_gate_w, L0_gnn_gate_b):
    import numpy as np
    import concourse.bacc as bacc
    from concourse.bass_utils import run_bass_kernel_spmd

    def arr(a):
        return np.ascontiguousarray(np.asarray(a))

    def edges(a, pad):
        a = np.asarray(a)
        return np.concatenate([a, np.full(P * EC - E, pad, a.dtype)]).reshape(P, EC)

    xp = np.concatenate([np.asarray(x), np.zeros((NP - N, H), np.float32)])
    twice = lambda a: np.tile(np.asarray(a), 2)
    f_b1, f_b2 = np.asarray(L0_gnn_filt_b1), np.asarray(L0_gnn_filt_b2)
    cols = np.stack([twice(L0_gnn_centers), twice(L0_gnn_widths), twice(L0_gnn_rbf_b1), f_b1[:P], f_b1[P:],
                     f_b2[:P], f_b2[P:], twice(L0_gnn_rbf_b2)], axis=1)
    rows = np.tile(np.concatenate([np.asarray(a) for a in (L0_gnn_filt_b3, L0_gnn_node_b, L0_gnn_gate_b)]), (3, 1))
    arrays = {
        "x": xp, "xT": arr(xp.T),
        "src": edges(src, PAD_NODE), "dst": edges(dst, PAD_NODE), "wgt": edges(edge_weight, 0.0),
        "cols": arr(cols), "rows": arr(rows), "ln_gb": np.stack([np.asarray(L0_gnn_ln_g), np.asarray(L0_gnn_ln_b)]),
        "w1": arr(L0_gnn_rbf_w1), "w2T": arr(np.tile(np.asarray(L0_gnn_rbf_w2).T, (1, 2))),
        "f1": arr(L0_gnn_filt_w1), "f2": arr(L0_gnn_filt_w2), "f3": arr(L0_gnn_filt_w3),
        "node_w": arr(L0_gnn_node_w), "gate_w": arr(L0_gnn_gate_w),
    }
    nc = bacc.Bacc("TRN2", target_bir_lowering=False, num_devices=1)
    args = [nc.dram_tensor(k, a.shape, mybir.dt.from_np(a.dtype), kind="ExternalInput").ap()
            for k, a in arrays.items()]
    out = nc.dram_tensor("out", (NP, H), mybir.dt.float32, kind="ExternalOutput").ap()
    build(nc, *args, out)
    result = run_bass_kernel_spmd(nc, [arrays], core_ids=[0])
    return result.results[0]["out"][:N]
```
